# Optimizing a Trainium2 kernel written in Bass

```python
import numpy as np
import jax
import jax.numpy as jnp

def _softmax(x, axis=-1):
    return jax.nn.softmax(x, axis=axis)

def _gelu(x):
    return jax.nn.gelu(x, approximate=True)

def _silu(x):
    return jax.nn.silu(x)

def _sigmoid(x):
    return jax.nn.sigmoid(x)

def _layernorm(x, axis=-1, eps=1e-05):
    m = jnp.mean(x, axis=axis, keepdims=True)
    v = jnp.var(x, axis=axis, keepdims=True)
    return (x - m) / jnp.sqrt(v + eps)

def _scatter_add(tgt, idx, src, axis=0):
    return tgt.at[idx].add(src)

def _segment_sum(src, seg, n):
    return jax.ops.segment_sum(src, seg, n)
kernel_name = 'mk_seq_postln_d1_jaxref_r4_4b3da6'

def setup_inputs(seed: int=0):
    np.random.seed(seed)
    _w = jnp.asarray

    def _L0_attn_setup():
        import jax, jax.numpy as jnp
        import numpy as np
        EMBED = 256
        HEADS = 16
        HDIM = EMBED // HEADS
        B, S = (4, 1024)
        key = jax.random.key(seed)
        ks = jax.random.split(key, 11)
        scale = 1.0 / np.sqrt(EMBED)

        def lin(k):
            return jax.random.uniform(k, (EMBED, EMBED), jnp.float32, -scale, scale)

        def bias(k):
            return jax.random.uniform(k, (EMBED,), jnp.float32, -scale, scale)
        return {'x': jax.random.normal(ks[0], (B, S, EMBED), jnp.float32), 'Wq': lin(ks[1]), 'bq': bias(ks[2]), 'Wk': lin(ks[3]), 'bk': bias(ks[4]), 'Wv': lin(ks[5]), 'bv': bias(ks[6]), 'Wg': lin(ks[7]), 'bg': bias(ks[8]), 'Wo': lin(ks[9]), 'bo': bias(ks[10])}
    _L0_attn_in = _L0_attn_setup()

    def _L0_ffn_setup():
        import jax, jax.numpy as jnp
        import numpy as np
        from jax import lax
        DIM = 256
        N_EXPERTS = 16
        TOPK = 4
        N_GROUPS = 4
        TOPK_GROUPS = 2
        ROUTE_SCALE = 1.0
        INTER = 128
        SHARED_INTER = 2 * INTER

        def _gate(x, gate_w):
            T = x.shape[0]
            logits = x @ gate_w.T
            scores = jax.nn.softmax(logits.astype(jnp.float32), axis=-1)
            original_scores = scores
            g = scores.reshape(T, N_GROUPS, N_EXPERTS // N_GROUPS)
            group_scores = g.max(axis=-1)
            _, gidx = lax.top_k(group_scores, TOPK_GROUPS)
            gmask = jnp.zeros_like(group_scores).at[jnp.arange(T)[:, None], gidx].set(1.0)
            masked = (g * gmask[..., None]).reshape(T, N_EXPERTS)
            _, indices = lax.top_k(masked, TOPK)
            weights = jnp.take_along_axis(original_scores, indices, axis=1)
            weights = weights * ROUTE_SCALE
            return (weights.astype(x.dtype), indices)
        key = jax.random.key(seed)
        ks = jax.random.split(key, 8)
        s = lambda fan_in: 1.0 / np.sqrt(fan_in)
        return {'x': jax.random.normal(ks[0], (2, 256, DIM), dtype=jnp.float32), 'gate_w': jax.random.normal(ks[1], (N_EXPERTS, DIM), dtype=jnp.float32) * s(DIM), 'w1': jax.random.normal(ks[2], (N_EXPERTS, DIM, INTER), dtype=jnp.float32) * s(DIM), 'w2': jax.random.normal(ks[3], (N_EXPERTS, INTER, DIM), dtype=jnp.float32) * s(INTER), 'w3': jax.random.normal(ks[4], (N_EXPERTS, DIM, INTER), dtype=jnp.float32) * s(DIM), 'ws1': jax.random.normal(ks[5], (DIM, SHARED_INTER), dtype=jnp.float32) * s(DIM), 'ws2': jax.random.normal(ks[6], (SHARED_INTER, DIM), dtype=jnp.float32) * s(SHARED_INTER), 'ws3': jax.random.normal(ks[7], (DIM, SHARED_INTER), dtype=jnp.float32) * s(DIM)}
    _L0_ffn_in = _L0_ffn_setup()
    _d = {'L0_attn_x': _L0_attn_in['x'], 'L0_attn_Wq': _L0_attn_in['Wq'], 'L0_attn_bq': _L0_attn_in['bq'], 'L0_attn_Wk': _L0_attn_in['Wk'], 'L0_attn_bk': _L0_attn_in['bk'], 'L0_attn_Wv': _L0_attn_in['Wv'], 'L0_attn_bv': _L0_attn_in['bv'], 'L0_attn_Wg': _L0_attn_in['Wg'], 'L0_attn_bg': _L0_attn_in['bg'], 'L0_attn_Wo': _L0_attn_in['Wo'], 'L0_attn_bo': _L0_attn_in['bo'], 'L0_ffn_gate_w': _L0_ffn_in['gate_w'], 'L0_ffn_w1': _L0_ffn_in['w1'], 'L0_ffn_w2': _L0_ffn_in['w2'], 'L0_ffn_w3': _L0_ffn_in['w3'], 'L0_ffn_ws1': _L0_ffn_in['ws1'], 'L0_ffn_ws2': _L0_ffn_in['ws2'], 'L0_ffn_ws3': _L0_ffn_in['ws3']}
    _x0 = _d['L0_attn_x']
    _d['L0_attn_x'] = jax.random.normal(jax.random.fold_in(jax.random.key(seed), 1), (8, 512, 256), dtype=_x0.dtype)
    del _x0
    return _d

def reference(L0_attn_x, L0_attn_Wq, L0_attn_bq, L0_attn_Wk, L0_attn_bk, L0_attn_Wv, L0_attn_bv, L0_attn_Wg, L0_attn_bg, L0_attn_Wo, L0_attn_bo, L0_ffn_gate_w, L0_ffn_w1, L0_ffn_w2, L0_ffn_w3, L0_ffn_ws1, L0_ffn_ws2, L0_ffn_ws3):

    def _L0_attn_ref(x, Wq, bq, Wk, bk, Wv, bv, Wg, bg, Wo, bo):
        import jax, jax.numpy as jnp
        import numpy as np
        EMBED = 256
        HEADS = 16
        HDIM = EMBED // HEADS
        B, S = (4, 1024)
        b, s, _ = x.shape

        def split_heads(t):
            return t.reshape(b, s, HEADS, HDIM).transpose(0, 2, 1, 3)
        q = split_heads(x @ Wq + bq)
        k = split_heads(x @ Wk + bk)
        v = split_heads(x @ Wv + bv)
        q = jax.nn.elu(q) + 1.0
        k = jax.nn.elu(k) + 1.0
        kv = jnp.einsum('bhsd,bhse->bhde', k, v)
        attn = jnp.einsum('bhsd,bhde->bhse', q, kv)
        attn = attn.transpose(0, 2, 1, 3).reshape(b, s, EMBED)
        gate = jax.nn.sigmoid(x @ Wg + bg)
        out = gate * attn @ Wo + bo
        return out

    def _L0_ffn_ref(x, gate_w, w1, w2, w3, ws1, ws2, ws3):
        import jax, jax.numpy as jnp
        import numpy as np
        from jax import lax
        DIM = 256
        N_EXPERTS = 16
        TOPK = 4
        N_GROUPS = 4
        TOPK_GROUPS = 2
        ROUTE_SCALE = 1.0
        INTER = 128
        SHARED_INTER = 2 * INTER

        def _gate(x, gate_w):
            T = x.shape[0]
            logits = x @ gate_w.T
            scores = jax.nn.softmax(logits.astype(jnp.float32), axis=-1)
            original_scores = scores
            g = scores.reshape(T, N_GROUPS, N_EXPERTS // N_GROUPS)
            group_scores = g.max(axis=-1)
            _, gidx = lax.top_k(group_scores, TOPK_GROUPS)
            gmask = jnp.zeros_like(group_scores).at[jnp.arange(T)[:, None], gidx].set(1.0)
            masked = (g * gmask[..., None]).reshape(T, N_EXPERTS)
            _, indices = lax.top_k(masked, TOPK)
            weights = jnp.take_along_axis(original_scores, indices, axis=1)
            weights = weights * ROUTE_SCALE
            return (weights.astype(x.dtype), indices)
        shape = x.shape
        xt = x.reshape(-1, DIM)
        T = xt.shape[0]
        weights, indices = _gate(xt, gate_w)
        c = jnp.zeros((T, N_EXPERTS), dtype=xt.dtype)
        c = c.at[jnp.arange(T)[:, None], indices].add(weights)
        h1 = jnp.einsum('td,edi->tei', xt, w1)
        h3 = jnp.einsum('td,edi->tei', xt, w3)
        a = jax.nn.silu(h1) * h3
        y = jnp.einsum('tei,eid,te->td', a, w2, c)
        z = jax.nn.silu(xt @ ws1) * (xt @ ws3) @ ws2
        return (y + z).reshape(shape)
    x = L0_attn_x
    x = _layernorm(x + _L0_attn_ref(x, L0_attn_Wq, L0_attn_bq, L0_attn_Wk, L0_attn_bk, L0_attn_Wv, L0_attn_bv, L0_attn_Wg, L0_attn_bg, L0_attn_Wo, L0_attn_bo), axis=-1)
    x = _layernorm(x + _L0_ffn_ref(x, L0_ffn_gate_w, L0_ffn_w1, L0_ffn_w2, L0_ffn_w3, L0_ffn_ws1, L0_ffn_ws2, L0_ffn_ws3), axis=-1)
    return x

_drawn_inputs = setup_inputs


def setup_inputs(seed=0):
    import zlib

    import numpy as np

    out = dict(_drawn_inputs(seed))
    spreads = {}
    factors = {'L0_attn_bq': 5.237, 'L0_attn_bk': 6.473, 'L0_attn_bo': 64.0}
    for name, (base, spread) in spreads.items():
        noise = np.random.default_rng([zlib.crc32(name.encode()), seed]).standard_normal(out[name].shape)
        drawn = base * np.exp(spread * noise) if base else spread * noise
        out[name] = jnp.asarray(drawn.astype(out[name].dtype))
    for name, factor in factors.items():
        out[name] = (out[name] * factor).astype(out[name].dtype)
    return out
```

```python
from contextlib import ExitStack

import concourse.bass as bass
from concourse import mybir

F32 = mybir.dt.float32
HI = mybir.dt.float16
LO = mybir.dt.bfloat16
ALU = mybir.AluOpType
ACT = mybir.ActivationFunctionType
AX_X = mybir.AxisListType.X

P = 128
LN_EPS = 1e-5
HDIM = 16
GROUPS = 4
TOP_GROUPS = 2
TOP_K = 4
TAKEN = -1.0
FILLER = -2.0

GATING_STEPS = 15


def attention_and_experts(nc: bass.Bass, x, Wq, bq, Wk, bk, Wv, bv, Wg, bg, Wo, bo,
                          gate_w, w1, w2, w3, ws1, ws2, ws3, out):
    NB, S, D = x.shape
    KC = D // P
    TT = S // P
    E, _, INTER = w1.shape
    SHARED = ws1.shape[1] // INTER
    NCH = SHARED + E
    PAIRS = NCH // 2
    RING = 4
    QUADS = E // RING
    assert (P, KC, TT, E, INTER, SHARED) == (128, 2, 4, 16, 128, 2) and NCH - SHARED == RING * QUADS
    assert NB >= 4 and PAIRS == NB + 1 and S == 512
    W13 = 2 * KC * INTER
    WCOLS = W13 + D
    EG = E // GROUPS

    c_dram = nc.dram_tensor("routing_scratch", (E, NB, S), F32, kind="Internal").ap()

    with ExitStack() as ctx:
        def sb(name, shape, dt=F32):
            return ctx.enter_context(nc.sbuf_tensor(name, shape, dt))

        def bank(name):
            return ctx.enter_context(nc.psum_tensor(name, [P, 512], F32))

        def sem(name):
            return ctx.enter_context(nc.semaphore(name))

        x_all = sb("x_all", [P, NB, TT, D])
        x_in = sb("x_in", [P, TT, D])
        x1_sb = sb("x1_sb", [P, TT, D])
        xT_hi = sb("xT_hi", [P, KC, NB, S], HI)
        xT_lo = sb("xT_lo", [P, KC, NB, S], LO)
        wa_hi = sb("wa_hi", [P, KC, 4 * D], HI)
        wa_lo = sb("wa_lo", [P, KC, 4 * D], LO)
        wo_sb = sb("wo_sb", [P, KC, D])
        we_hi = sb("we_hi", [P, NCH, WCOLS], HI)
        we_lo = sb("we_lo", [P, NCH, WCOLS], LO)
        stage = sb("stage", [P, 2, WCOLS])
        cb = sb("cb", [P, RING, S])
        wa_stage = cb[:].rearrange("p r s -> p (r s)").rearrange("p (c n) -> p c n", c=KC)
        ident = sb("ident", [P, P])
        head_mask = sb("head_mask", [P, KC, P])
        earlier = sb("earlier", [P, TT, GROUPS, GROUPS])
        minus_half = sb("minus_half", [P, TT])
        eps = sb("eps", [P, TT])
        b_kv = sb("b_kv", [P, 2 * D])
        b_o = sb("b_o", [P, D])
        b_q = sb("b_q", [P, KC])
        b_g = sb("b_g", [P, KC])
        gw_sb = sb("gw_sb", [E, D])
        gwT_hi = sb("gwT_hi", [P, KC, E], HI)
        gwT_lo = sb("gwT_lo", [P, KC, E], LO)
        kv = sb("kv", [P, TT, 2 * D])
        k_min = sb("k_min", [P, TT, D])
        q_min = sb("q_min", [P, KC, S])
        q_fm = sb("q_fm", [P, KC, S])
        gate = sb("gate", [P, KC, S])
        gated = sb("gated", [P, KC, S])
        kv_heads = sb("kv_heads", [P, KC, P])
        wait_pad = sb("wait_pad", [P, 1])
        bn = sb("bn", [P, TT, 6])
        mv = sb("mv", [P, TT, 2])
        var_eps = sb("var_eps", [P, TT])
        rstd = sb("rstd", [P, TT])
        r_max = sb("r_max", [P, TT])
        r_sub = sb("r_sub", [P, TT, E])
        r_exp = sb("r_exp", [P, TT, E])
        r_sum = sb("r_sum", [P, TT])
        r_inv = sb("r_inv", [P, TT])
        score = sb("score", [P, TT, E])
        g_max = sb("g_max", [P, TT, GROUPS])
        g_gt = sb("g_gt", [P, TT, GROUPS, GROUPS])
        g_eq = sb("g_eq", [P, TT, GROUPS, GROUPS])
        g_rank = sb("g_rank", [P, TT, GROUPS])
        g_sel = sb("g_sel", [P, TT, GROUPS])
        masked = sb("masked", [P, TT, E + 8 - TOP_K])
        top8 = sb("top8", [P, TT, 8])
        marked = sb("marked", [P, TT, E + 8 - TOP_K])
        c_tok = sb("c_tok", [P, TT, E])
        cT = sb("cT", [E, S])
        s_act = sb("s_act", [P, S])
        s_c = sb("s_c", [P, S])
        a_act = sb("a_act", [P, S])
        a_hi = [sb(f"a_hi{p}", [P, S], HI) for p in range(2)]
        a_lo = [sb(f"a_lo{p}", [P, S], LO) for p in range(2)]
        yT = sb("yT", [P, KC, S])
        o_sb = sb("o_sb", [P, TT, D])

        h_banks = [[bank("h1_even"), bank("h3_even")], [bank("h1_odd"), bank("h3_odd")]]
        kv_bank = h_banks[0]
        qg_bank = h_banks[1]
        y_bank = [bank("y0"), bank("y1")]
        t_bank = [bank("t0"), bank("t1")]

        x_loaded, wa_loaded, small_loaded = sem("x_loaded"), sem("wa_loaded"), sem("small_loaded")
        stage_loaded, ct_stored, out_stored = sem("stage_loaded"), sem("ct_stored"), sem("out_stored")
        cb_loaded = [sem(f"cb_loaded{r}") for r in range(RING)]
        const_step, const_ready = sem("const_step"), sem("const_ready")
        wa_hi_ready, wa_lo_ready = sem("wa_hi_ready"), sem("wa_lo_ready")
        gw_transposed, gw_hi_ready, gw_lo_ready = sem("gw_transposed"), sem("gw_hi_ready"), sem("gw_lo_ready")
        we_hi_ready, we_lo_ready = sem("we_hi_ready"), sem("we_lo_ready")
        x_transposed, xt_hi_ready, xt_lo_ready = sem("x_transposed"), sem("xt_hi_ready"), sem("xt_lo_ready")
        kv_projected, kv_biased = sem("kv_projected"), sem("kv_biased")
        k_min_ready, k_exp_ready, k_ready = sem("k_min_ready"), sem("k_exp_ready"), sem("k_ready")
        q_projected, q_min_ready, q_relu_ready = sem("q_projected"), sem("q_min_ready"), sem("q_relu_ready")
        q_exp_ready, q_ready = sem("q_exp_ready"), sem("q_ready")
        g_projected, gate_ready = sem("g_projected"), sem("gate_ready")
        kv_summed, kv_heads_ready = sem("kv_summed"), sem("kv_heads_ready")
        attended, gated_ready = sem("attended"), sem("gated_ready")
        wo_projected, x_biased, residual_ready = sem("wo_projected"), sem("x_biased"), sem("residual_ready")
        bn_ready, mv_ready, var_eps_ready, rstd_ready = sem("bn_ready"), sem("mv_ready"), sem("var_eps_ready"), sem("rstd_ready")
        x1_ready, x1_transposed, x1_kept = sem("x1_ready"), sem("x1_transposed"), sem("x1_kept")
        x1t_hi_ready, x1t_lo_ready = sem("x1t_hi_ready"), sem("x1t_lo_ready")
        logits_ready, gating_step, r_exp_ready = sem("logits_ready"), sem("gating_step"), sem("r_exp_ready")
        c_ready, c_transposed, ct_copied = sem("c_ready"), sem("c_transposed"), sem("ct_copied")
        h1_ready, h3_ready, silu_ready = sem("h1_ready"), sem("h3_ready"), sem("silu_ready")
        sc_ready, a_ready, a_hi_ready, a_lo_ready = sem("sc_ready"), sem("a_ready"), sem("a_hi_ready"), sem("a_lo_ready")
        down_done = sem("down_done")
        y0_copied, y1_copied, y_transposed = sem("y0_copied"), sem("y1_copied"), sem("y_transposed")
        out_ready = sem("out_ready")

        def stage_sources(m):
            if isinstance(m, int) and m == 0:
                return [(ws1[:, s * INTER:(s + 1) * INTER], ws3[:, s * INTER:(s + 1) * INTER],
                         ws2[s * INTER:(s + 1) * INTER, :]) for s in range(SHARED)]
            return [(w1[2 * m - 2 + s], w3[2 * m - 2 + s], w2[2 * m - 2 + s]) for s in range(2)]

        block = ctx.enter_context(nc.Block())

        @block.sync
        def _(sp):
            def load_x(b):
                sp.dma_start(x_in[:, :, :], x[b].rearrange("(t p) d -> p t d", p=P)).then_inc(x_loaded, 16)

            def load_stage(m):
                for s, (a1, a3, a2) in enumerate(stage_sources(m)):
                    for k, src in enumerate((a1, a3)):
                        dst = stage[:, s, k * KC * INTER:(k + 1) * KC * INTER]
                        sp.dma_start(dst.rearrange("p (c i) -> p c i", c=KC),
                                     src.rearrange("(c p) i -> p c i", p=P)).then_inc(stage_loaded, 16)
                    sp.dma_start(stage[:, s, W13:], a2).then_inc(stage_loaded, 16)

            def store_cT(b):
                sp.wait_ge(ct_copied, b + 1)
                sp.dma_start(c_dram[:, b, :], cT[:, :]).then_inc(ct_stored, 16)

            load_x(0)
            for k, w in enumerate((Wk, Wv, Wq, Wg)):
                sp.dma_start(wa_stage[:, :, k * D:(k + 1) * D],
                             w.rearrange("(c p) n -> p c n", p=P)).then_inc(wa_loaded, 16)
            sp.dma_start(b_kv[:, 0:D], bk.partition_broadcast(P)).then_inc(small_loaded, 16)
            sp.dma_start(b_kv[:, D:], bv.partition_broadcast(P)).then_inc(small_loaded, 16)
            sp.dma_start(b_o[:, :], bo.partition_broadcast(P)).then_inc(small_loaded, 16)
            sp.dma_start(wo_sb[:, :, :], Wo.rearrange("(c p) n -> p c n", p=P)).then_inc(small_loaded, 16)
            sp.dma_start(gw_sb[:, :], gate_w).then_inc(small_loaded, 16)
            load_stage(0)

            def batch(b, has_c, has_x):
                if has_x:
                    sp.wait_ge(x_biased, b + 1)
                    load_x(b + 1)
                if has_c:
                    store_cT(b - 2)
                sp.wait_ge(we_lo_ready, b + 1)
                load_stage(b + 1)

            batch(0, False, True)
            batch(1, False, True)
            with sp.Fori(2, NB - 1) as b:
                batch(b, True, True)
            batch(NB - 1, True, False)
            store_cT(NB - 2)

            def load_cb(n, q, r, wait):
                if wait:
                    sp.wait_ge(sc_ready, E * n + RING * (q - 1) + r + 1)
                sp.dma_start(cb[:, r, :], c_dram[RING * q + r, n, :].partition_broadcast(P)).then_inc(cb_loaded[r], 16)

            def store_out(n):
                sp.wait_ge(out_ready, n + 1)
                sp.dma_start(out[n].rearrange("(t p) d -> p t d", p=P), o_sb[:, :, :]).then_inc(out_stored, 16)

            sp.wait_ge(ct_stored, 16)
            for r in range(RING):
                load_cb(0, 0, r, False)
            with sp.Fori(1, QUADS) as q:
                for r in range(RING):
                    load_cb(0, q, r, True)
            store_cT(NB - 1)
            with sp.Fori(1, NB) as n:
                sp.wait_ge(ct_stored, 16 * (n + 1))
                for r in range(RING):
                    sp.wait_ge(sc_ready, E * n - RING + r + 1)
                    sp.dma_start(cb[:, r, :], c_dram[r, n, :].partition_broadcast(P)).then_inc(cb_loaded[r], 16)
                store_out(n - 1)
                with sp.Fori(1, QUADS) as q:
                    for r in range(RING):
                        load_cb(n, q, r, True)
            store_out(NB - 1)
            sp.wait_ge(out_stored, 16 * NB)

        @block.gpsimd
        def _(pool):
            pool.memset(ident[:, :], 0.0).then_inc(const_step, 1)
            pool.memset(head_mask[:, :, :], 1.0).then_inc(const_step, 1)
            pool.memset(earlier[:, :, :, :], 1.0).then_inc(const_step, 1)
            pool.memset(minus_half[:, :], -0.5).then_inc(const_ready, 1)
            pool.memset(eps[:, :], LN_EPS).then_inc(const_ready, 1)
            pool.memset(masked[:, :, E:], FILLER).then_inc(const_ready, 1)
            pool.wait_ge(const_step, 3)
            pool.affine_select(out=ident[:, :], in_=ident[:, :], compare_op=ALU.not_equal, fill=1.0,
                               base=0, pattern=[[-1, P]], channel_multiplier=1).then_inc(const_ready, 1)
            pool.affine_select(out=earlier[:, :, :, :], in_=earlier[:, :, :, :], compare_op=ALU.is_ge, fill=0.0,
                               base=-1, pattern=[[0, TT], [1, GROUPS], [-1, GROUPS]],
                               channel_multiplier=0).then_inc(const_ready, 1)
            heads = head_mask[:, :, :].rearrange("p c (h e) -> p c h e", e=HDIM)
            pool.affine_select(out=heads, in_=heads, compare_op=ALU.is_ge, fill=0.0, base=0,
                               pattern=[[0, KC], [-HDIM, P // HDIM], [0, HDIM]],
                               channel_multiplier=1).then_inc(const_step, 1)
            pool.wait_ge(const_step, 4)
            pool.affine_select(out=heads, in_=heads, compare_op=ALU.is_ge, fill=0.0, base=HDIM - 1,
                               pattern=[[0, KC], [HDIM, P // HDIM], [0, HDIM]],
                               channel_multiplier=-1).then_inc(const_ready, 1)
            pool.wait_ge(const_ready, 6)
            pool.wait_ge(small_loaded, 16 * 7)

            def x_plus_bias(b):
                pool.wait_ge(x_transposed, KC * (b + 1))
                for t in range(TT):
                    last = pool.tensor_tensor(x_all[:, b, t, :], x_in[:, t, :], b_o[:, :], ALU.add)
                last.then_inc(x_biased, 1)

            def rstd_of(ln):
                pool.wait_ge(mv_ready, ln + 1)
                pool.tensor_tensor(var_eps[:, :], mv[:, :, 1], eps[:, :], ALU.add).then_inc(var_eps_ready, 1)
                pool.wait_ge(var_eps_ready, ln + 1)
                pool.tensor_tensor(rstd[:, :], var_eps[:, :], minus_half[:, :], ALU.pow).then_inc(rstd_ready, 1)

            def split_lo(m):
                pool.wait_ge(we_hi_ready, m + 1)
                for s in range(2):
                    c = 2 * m + s
                    last = pool.tensor_tensor(we_lo[:, c, :], stage[:, s, :], we_hi[:, c, :], ALU.subtract)
                last.then_inc(we_lo_ready, 1)

            def batch(b, has_prev):
                x_plus_bias(b)
                if has_prev:
                    rstd_of(b - 1)
                for c in range(KC):
                    pool.wait_ge(q_exp_ready, KC * b + c + 1)
                    pool.tensor_tensor(q_fm[:, c, :], q_fm[:, c, :], q_min[:, c, :], ALU.add).then_inc(q_ready, 1)
                split_lo(b)

            batch(0, False)
            with pool.Fori(1, NB) as b:
                batch(b, True)
            split_lo(NB)
            with pool.Fori(NB - 1, 2 * NB) as ln:
                rstd_of(ln)

        @block.scalar
        def _(act):
            act.dma_start(b_q[:, :], bq.rearrange("(c p) -> p c", p=P), allow_slow_non_contiguous=True).then_inc(small_loaded, 16)
            act.dma_start(b_g[:, :], bg.rearrange("(c p) -> p c", p=P), allow_slow_non_contiguous=True).then_inc(small_loaded, 16)

            def xt_hi(b):
                for c in range(KC):
                    act.wait_ge(x_transposed, KC * b + c + 1)
                    act.activation(xT_hi[:, c, b, :], t_bank[c][:, :], ACT.Copy).then_inc(xt_hi_ready, 1)

            def x1t_hi(b):
                for c in range(KC):
                    act.wait_ge(x1_transposed, KC * b + c + 1)
                    act.activation(xT_hi[:, c, b, :], t_bank[c][:, :], ACT.Copy).then_inc(x1t_hi_ready, 1)

            def keep_x1(b):
                act.wait_ge(x1_ready, b + 1)
                act.activation(x_all[:, b, :, :], x1_sb[:, :, :], ACT.Copy).then_inc(x1_kept, 1)

            def split_hi(m):
                act.wait_ge(stage_loaded, 16 * 6 * (m + 1))
                act.activation(we_hi[:, 2 * m, :], stage[:, 0, :], ACT.Copy)
                act.activation(we_hi[:, 2 * m + 1, :], stage[:, 1, :], ACT.Copy).then_inc(we_hi_ready, 1)

            def routing_exp(b):
                act.wait_ge(gating_step, GATING_STEPS * b + 2)
                act.activation(r_exp[:, :, :], r_sub[:, :, :], ACT.Exp).then_inc(r_exp_ready, 1)

            def cT_copy(b, has_prev):
                act.wait_ge(c_transposed, b + 1)
                if has_prev:
                    act.wait_ge(ct_stored, 16 * b)
                act.activation(cT[:, :], t_bank[0][0:E, :], ACT.Copy).then_inc(ct_copied, 1)

            def batch(b, prev, c_prev, nxt):
                if c_prev:
                    routing_exp(b - 2)
                    cT_copy(b - 2, c_prev == 2)
                split_hi(b)
                if nxt:
                    xt_hi(b + 1)
                act.wait_ge(small_loaded, 16 * 7)

                def q_relu(c):
                    act.wait_ge(q_projected, KC * b + c + 1)
                    if prev:
                        act.wait_ge(attended, KC * b)
                    act.activation(q_fm[:, c, :], qg_bank[c][:, :], ACT.Relu, bias=b_q[:, c:c + 1]).then_inc(q_relu_ready, 1)

                def q_expo(c):
                    act.wait_ge(q_min_ready, KC * b + c + 1)
                    act.wait_ge(q_relu_ready, KC * b + c + 1)
                    act.activation(q_min[:, c, :], q_min[:, c, :], ACT.Exp).then_inc(q_exp_ready, 1)

                q_relu(0)
                act.wait_ge(k_min_ready, b + 1)
                act.activation(k_min[:, :, :], k_min[:, :, :], ACT.Exp).then_inc(k_exp_ready, 1)
                q_expo(0)
                q_relu(1)
                if prev:
                    x1t_hi(b - 1)
                q_expo(1)
                if prev:
                    keep_x1(b - 1)
                for c in range(KC):
                    act.wait_ge(g_projected, KC * b + c + 1)
                    if prev:
                        act.wait_ge(gated_ready, KC * b)
                    act.activation(gate[:, c, :], qg_bank[c][:, :], ACT.Sigmoid, bias=b_g[:, c:c + 1]).then_inc(gate_ready, 1)

            xt_hi(0)
            act.wait_ge(wa_loaded, 16 * 4)
            act.activation(wa_hi[:, :, 0:2 * D], wa_stage[:, :, 0:2 * D], ACT.Copy).then_inc(wa_hi_ready, 1)
            act.activation(wa_hi[:, :, 2 * D:], wa_stage[:, :, 2 * D:], ACT.Copy).then_inc(wa_hi_ready, 1)
            act.wait_ge(gw_transposed, 1)
            act.activation(gwT_hi[:, :, :], y_bank[0][:, 0:KC * E].rearrange("p (c e) -> p c e", c=KC),
                           ACT.Copy).then_inc(gw_hi_ready, 1)
            batch(0, False, 0, True)
            batch(1, True, 0, True)
            batch(2, True, 1, True)
            with act.Fori(3, NB - 1) as b:
                batch(b, True, 2, True)
            batch(NB - 1, True, 2, False)
            routing_exp(NB - 2)
            split_hi(NB)

            def silu(g, has_prev=True):
                act.wait_ge(h1_ready, g + 1)
                if has_prev:
                    act.wait_ge(a_ready, g)
                act.activation(s_act[:, :], h_of(g)[0][:, :], ACT.Silu).then_inc(silu_ready, 1)

            def upper(g, reused=True):
                act.wait_ge(a_ready, g + 1)
                if reused:
                    act.wait_ge(down_done, g - 1)
                act.activation(slot_of(g, a_hi)[:, :], a_act[:, :], ACT.Copy).then_inc(a_hi_ready, 1)

            parity = [0]

            def h_of(_g):
                return h_banks[parity[0]]

            def slot_of(_g, pair):
                return pair[parity[0]]

            def block_of(n, first):
                g = NCH * n
                parity[0] = 0
                silu(g, not first)
                upper(g, not first)
                if not first:
                    if isinstance(n, int):
                        cT_copy(NB - 1, True)
                    act.wait_ge(down_done, g)
                    if not isinstance(n, int):
                        act.wait_ge(y_transposed, 2 * (n - 1))
                    act.activation(yT[:, 0, :], y_bank[0][:, :], ACT.Copy).then_inc(y0_copied, 1)
                parity[0] = 1
                silu(g + 1)
                if first:
                    cT_copy(NB - 2, True)
                upper(g + 1, not first)
                if first:
                    x1t_hi(NB - 1)
                    keep_x1(NB - 1)
                with act.Fori(0, QUADS) as q:
                    for r in range(RING):
                        parity[0] = r % 2
                        silu(g + SHARED + RING * q + r)
                        upper(g + SHARED + RING * q + r)

            block_of(0, True)
            routing_exp(NB - 1)
            block_of(1, False)
            with act.Fori(2, NB) as n:
                block_of(n, False)
            act.wait_ge(down_done, NCH * NB)
            act.wait_ge(y_transposed, 2 * (NB - 1))
            act.activation(yT[:, 0, :], y_bank[0][:, :], ACT.Copy).then_inc(y0_copied, 1)

        @block.vector
        def _(dve):
            def xt_lo(b):
                for c in range(KC):
                    dve.wait_ge(xt_hi_ready, KC * b + c + 1)
                    dve.tensor_tensor(xT_lo[:, c, b, :], t_bank[c][:, :], xT_hi[:, c, b, :],
                                      ALU.subtract).then_inc(xt_lo_ready, 1)

            def x1t_lo(b):
                for c in range(KC):
                    dve.wait_ge(x1t_hi_ready, KC * b + c + 1)
                    dve.tensor_tensor(xT_lo[:, c, b, :], t_bank[c][:, :], xT_hi[:, c, b, :],
                                      ALU.subtract).then_inc(x1t_lo_ready, 1)

            def kv_bias(b, t, prev):
                dve.wait_ge(kv_projected, TT * b + t + 1)
                if prev:
                    dve.wait_ge(kv_summed, b)
                dve.tensor_tensor(kv[:, t, :], kv_bank[t % 2][:, :], b_kv[:, :], ALU.add).then_inc(kv_biased, 1)

            def apply_gate(b, has_prev):
                for c in range(KC):
                    dve.wait_ge(attended, KC * b + c + 1)
                    dve.wait_ge(gate_ready, KC * b + c + 1)
                    if has_prev:
                        dve.wait_ge(wo_projected, 2 * b)
                    dve.tensor_tensor(gated[:, c, :], y_bank[c][:, :], gate[:, c, :], ALU.mult).then_inc(gated_ready, 1)

            def norm_stats(rows, ln):
                for t in range(TT):
                    last = dve.bn_stats(bn[:, t, :], rows(t))
                last.then_inc(bn_ready, 1)
                dve.wait_ge(bn_ready, ln + 1)
                dve.memset(wait_pad[:, :], 0.0)
                for t in range(TT):
                    last = dve.bn_aggr(mv[:, t, :], bn[:, t, :])
                last.then_inc(mv_ready, 1)

            def normalize(rows, ln, done):
                dve.wait_ge(rstd_ready, ln + 1)
                for t in range(TT):
                    last = dve.tensor_scalar(rows(t), rows(t), mv[:, t, 0:1], rstd[:, t:t + 1],
                                             ALU.subtract, ALU.mult)
                last.then_inc(done, 1)

            def residual(b, has_prev):
                dve.wait_ge(x_biased, b + 1)
                if has_prev:
                    dve.wait_ge(x1_transposed, KC * b)
                    dve.wait_ge(x1_kept, b)
                for h in range(2):
                    dve.wait_ge(wo_projected, 2 * b + h + 1)
                    dve.tensor_tensor(x1_sb[:, 2 * h:2 * h + 2, :],
                                      y_bank[h][:, :].rearrange("p (t d) -> p t d", t=2),
                                      x_all[:, b, 2 * h:2 * h + 2, :], ALU.add).then_inc(residual_ready, 1)
                dve.wait_ge(residual_ready, 2 * b + 2)
                norm_stats(lambda t: x1_sb[:, t, :], b)

            def routing_head(b):
                at = GATING_STEPS * b
                logits = t_bank[1][:, 0:TT * E].rearrange("p (t e) -> p t e", t=TT)
                per_tile = [P, TT, E]
                dve.wait_ge(logits_ready, b + 1)
                dve.tensor_reduce(r_max[:, :], logits, AX_X, ALU.max).then_inc(gating_step, 1)
                dve.wait_ge(gating_step, at + 1)
                dve.tensor_tensor(r_sub[:, :, :], logits, r_max[:, :].unsqueeze(2).to_broadcast(per_tile),
                                  ALU.subtract).then_inc(gating_step, 1)

            def routing_tail(b, has_prev):
                at = GATING_STEPS * b
                per_tile = [P, TT, E]
                dve.wait_ge(r_exp_ready, b + 1)
                dve.tensor_reduce(r_sum[:, :], r_exp[:, :, :], AX_X, ALU.add).then_inc(gating_step, 1)
                dve.wait_ge(gating_step, at + 3)
                dve.reciprocal(r_inv[:, :], r_sum[:, :]).then_inc(gating_step, 1)
                dve.wait_ge(gating_step, at + 4)
                dve.tensor_tensor(score[:, :, :], r_exp[:, :, :], r_inv[:, :].unsqueeze(2).to_broadcast(per_tile),
                                  ALU.mult).then_inc(gating_step, 1)
                dve.wait_ge(gating_step, at + 5)
                grouped = score[:, :, :].rearrange("p t (g e) -> p t g e", g=GROUPS)
                dve.tensor_reduce(g_max[:, :, :], grouped, AX_X, ALU.max).then_inc(gating_step, 1)
                dve.wait_ge(gating_step, at + 6)
                pairs = [P, TT, GROUPS, GROUPS]
                other = g_max[:, :, :].unsqueeze(2).to_broadcast(pairs)
                own = g_max[:, :, :].unsqueeze(3).to_broadcast(pairs)
                dve.tensor_tensor(g_gt[:, :, :, :], other, own, ALU.is_gt)
                dve.tensor_tensor(g_eq[:, :, :, :], other, own, ALU.is_equal).then_inc(gating_step, 1)
                dve.wait_ge(gating_step, at + 7)
                dve.tensor_tensor(g_eq[:, :, :, :], g_eq[:, :, :, :], earlier[:, :, :, :], ALU.mult).then_inc(gating_step, 1)
                dve.wait_ge(gating_step, at + 8)
                dve.tensor_tensor(g_gt[:, :, :, :], g_gt[:, :, :, :], g_eq[:, :, :, :], ALU.add).then_inc(gating_step, 1)
                dve.wait_ge(gating_step, at + 9)
                dve.tensor_reduce(g_rank[:, :, :], g_gt[:, :, :, :], AX_X, ALU.add).then_inc(gating_step, 1)
                dve.wait_ge(gating_step, at + 10)
                dve.tensor_scalar(g_sel[:, :, :], g_rank[:, :, :], float(TOP_GROUPS), None, ALU.is_lt).then_inc(gating_step, 1)
                dve.wait_ge(gating_step, at + 11)
                dve.tensor_tensor(masked[:, :, 0:E].rearrange("p t (g e) -> p t g e", g=GROUPS), grouped,
                                  g_sel[:, :, :].unsqueeze(3).to_broadcast([P, TT, GROUPS, EG]),
                                  ALU.mult).then_inc(gating_step, 1)
                dve.wait_ge(gating_step, at + 12)
                dve.memset(wait_pad[:, :], 0.0)
                for t in range(TT):
                    last = dve.max(top8[:, t, :], masked[:, t, 0:E])
                last.then_inc(gating_step, 1)
                dve.wait_ge(gating_step, at + 13)
                dve.memset(top8[:, :, TOP_K:], FILLER).then_inc(gating_step, 1)
                dve.wait_ge(gating_step, at + 14)
                dve.memset(wait_pad[:, :], 0.0)
                for t in range(TT):
                    last = dve.match_replace(marked[:, t, :], top8[:, t, :], masked[:, t, :], TAKEN)
                last.then_inc(gating_step, 1)
                dve.wait_ge(gating_step, at + 15)
                if has_prev:
                    dve.wait_ge(c_transposed, b)
                dve.scalar_tensor_tensor(c_tok[:, :, :], marked[:, :, 0:E], TAKEN, score[:, :, :],
                                         ALU.is_equal, ALU.mult).then_inc(c_ready, 1)

            def batch(b, prev, prev2, nxt):
                if prev:
                    apply_gate(b - 1, prev2 > 0)
                if prev2:
                    routing_tail(b - 2, prev2 > 1)
                kv_bias(b, 0, prev)
                kv_bias(b, 1, prev)
                if prev:
                    residual(b - 1, prev2 > 0)
                kv_bias(b, 2, prev)
                kv_bias(b, 3, prev)
                dve.wait_ge(kv_biased, TT * (b + 1))
                dve.tensor_scalar(k_min[:, :, :], kv[:, :, 0:D], 0.0, None, ALU.min).then_inc(k_min_ready, 1)
                if prev:
                    normalize(lambda t: x1_sb[:, t, :], b - 1, x1_ready)
                if nxt:
                    xt_lo(b + 1)

                def q_minimum(c):
                    dve.wait_ge(q_relu_ready, KC * b + c + 1)
                    if prev:
                        dve.wait_ge(q_ready, KC * b)
                    dve.tensor_scalar(q_min[:, c, :], qg_bank[c][:, :], b_q[:, c:c + 1], 0.0,
                                      ALU.add, ALU.min).then_inc(q_min_ready, 1)

                q_minimum(0)
                dve.wait_ge(k_exp_ready, b + 1)
                dve.scalar_tensor_tensor(kv[:, :, 0:D], kv[:, :, 0:D], 0.0, k_min[:, :, :],
                                         ALU.max, ALU.add).then_inc(k_ready, 1)
                q_minimum(1)
                if prev:
                    x1t_lo(b - 1)
                dve.wait_ge(kv_summed, b + 1)
                if prev:
                    dve.wait_ge(attended, KC * b)
                dve.tensor_tensor(kv_heads[:, :, :], kv_bank[0][:, 0:KC * P].rearrange("p (c n) -> p c n", c=KC),
                                  head_mask[:, :, :], ALU.mult).then_inc(kv_heads_ready, 1)
                if prev:
                    routing_head(b - 1)

            dve.wait_ge(const_ready, 6)
            dve.wait_ge(small_loaded, 16 * 7)
            xt_lo(0)
            for k in range(2):
                half = slice(2 * D * k, 2 * D * (k + 1))
                dve.wait_ge(wa_hi_ready, k + 1)
                dve.tensor_tensor(wa_lo[:, :, half], wa_stage[:, :, half], wa_hi[:, :, half],
                                  ALU.subtract).then_inc(wa_lo_ready, 1)
            dve.wait_ge(gw_hi_ready, 1)
            dve.tensor_tensor(gwT_lo[:, :, :], y_bank[0][:, 0:KC * E].rearrange("p (c e) -> p c e", c=KC),
                              gwT_hi[:, :, :], ALU.subtract).then_inc(gw_lo_ready, 1)
            batch(0, False, 0, True)
            batch(1, True, 0, True)
            batch(2, True, 1, True)
            with dve.Fori(3, NB - 1) as b:
                batch(b, True, 2, True)
            batch(NB - 1, True, 2, False)
            apply_gate(NB - 1, True)
            routing_tail(NB - 2, True)

            def hidden(g, par, sc_count=None, ring=None, first=False):
                dve.wait_ge(silu_ready, g + 1)
                s = s_act
                if sc_count is not None:
                    slot, loads = ring
                    dve.wait_ge(cb_loaded[slot], 16 * loads)
                    dve.tensor_tensor(s_c[:, :], s_act[:, :], cb[:, slot, :], ALU.mult).then_inc(sc_ready, 1)
                    dve.wait_ge(sc_ready, sc_count)
                    s = s_c
                dve.wait_ge(h3_ready, g + 1)
                if not first:
                    dve.wait_ge(a_lo_ready, g)
                dve.tensor_tensor(a_act[:, :], h_banks[par][1][:, :], s[:, :], ALU.mult).then_inc(a_ready, 1)
                dve.wait_ge(a_hi_ready, g + 1)
                dve.tensor_tensor(a_lo[par][:, :], a_act[:, :], a_hi[par][:, :], ALU.subtract).then_inc(a_lo_ready, 1)

            def y_copy(n):
                dve.wait_ge(down_done, NCH * (n + 1))
                if not (isinstance(n, int) and n == 0):
                    dve.wait_ge(y_transposed, 2 * n)
                dve.tensor_copy(yT[:, 1, :], y_bank[1][:, :]).then_inc(y1_copied, 1)

            def finish(n):
                dve.wait_ge(x1_kept, n + 1)
                if not (isinstance(n, int) and n == 0):
                    dve.wait_ge(out_stored, 16 * n)
                for h in range(2):
                    dve.wait_ge(y_transposed, 2 * n + h + 1)
                    last = dve.tensor_tensor(o_sb[:, 2 * h:2 * h + 2, :],
                                             t_bank[h][:, :].rearrange("p (t d) -> p t d", t=2),
                                             x_all[:, n, 2 * h:2 * h + 2, :], ALU.add)
                    last.then_inc(residual_ready, 1)
                dve.wait_ge(residual_ready, 2 * (NB + n) + 2)
                norm_stats(lambda t: o_sb[:, t, :], NB + n)
                normalize(lambda t: o_sb[:, t, :], NB + n, out_ready)

            def block_of(n, first):
                g = NCH * n
                hidden(g, 0, first=first)
                if first:
                    residual(NB - 1, True)
                    normalize(lambda t: x1_sb[:, t, :], NB - 1, x1_ready)
                else:
                    y_copy(n - 1)
                hidden(g + 1, 1)
                if first:
                    x1t_lo(NB - 1)
                else:
                    finish(n - 1)
                with dve.Fori(0, QUADS) as q:
                    for r in range(RING):
                        hidden(g + SHARED + RING * q + r, r % 2, E * n + RING * q + r + 1,
                               (r, QUADS * n + q + 1))

            block_of(0, True)
            routing_head(NB - 1)
            routing_tail(NB - 1, True)
            block_of(1, False)
            with dve.Fori(2, NB) as n:
                block_of(n, False)
            y_copy(NB - 1)
            finish(NB - 1)

        @block.tensor
        def _(pe):
            def product(dst, sta_hi, sta_lo, mov_hi, mov_lo, start, stop):
                pe.matmul(dst, sta_hi, mov_hi, start=start, stop=False)
                pe.matmul(dst, sta_hi, mov_lo, start=False, stop=False)
                return pe.matmul(dst, sta_lo, mov_hi, start=False, stop=stop)

            def transpose_x(src, done):
                for c in range(KC):
                    for t in range(TT):
                        last = pe.transpose(t_bank[c][:, t * P:(t + 1) * P], src[:, t, c * P:(c + 1) * P],
                                            ident[:, :])
                    last.then_inc(done, 1)

            def project_kv(b, t):
                if not (isinstance(b, int) and b == 0) or t >= 2:
                    pe.wait_ge(kv_biased, TT * b + t - 1)
                if not (isinstance(b, int) and b == 0) and t == 0:
                    pe.wait_ge(kv_heads_ready, b)
                tok = slice(t * P, (t + 1) * P)
                for c in range(KC):
                    last = product(kv_bank[t % 2][:, :], xT_hi[:, c, b, tok], xT_lo[:, c, b, tok],
                                   wa_hi[:, c, 0:2 * D], wa_lo[:, c, 0:2 * D], c == 0, c == KC - 1)
                last.then_inc(kv_projected, 1)

            def project_features(b, m, col, done):
                cols = slice(col + m * P, col + (m + 1) * P)
                for c in range(KC):
                    last = product(qg_bank[m][:, :], wa_hi[:, c, cols], wa_lo[:, c, cols],
                                   xT_hi[:, c, b, :], xT_lo[:, c, b, :], c == 0, c == KC - 1)
                last.then_inc(done, 1)

            def project_out(b):
                for h in range(2):
                    pe.wait_ge(gated_ready, KC * (b + 1))
                    for t in range(2 * h, 2 * h + 2):
                        for c in range(KC):
                            last = pe.matmul(y_bank[h][:, (t % 2) * D:(t % 2 + 1) * D],
                                             gated[:, c, t * P:(t + 1) * P], wo_sb[:, c, :],
                                             start=c == 0, stop=c == KC - 1)
                    last.then_inc(wo_projected, 1)

            def sum_kv(b):
                pe.wait_ge(k_ready, b + 1)
                for c in range(KC):
                    for t in range(TT):
                        last = pe.matmul(kv_bank[0][:, c * P:(c + 1) * P], kv[:, t, c * P:(c + 1) * P],
                                         kv[:, t, D + c * P:D + (c + 1) * P], start=t == 0, stop=t == TT - 1)
                last.then_inc(kv_summed, 1)

            def attend(b):
                pe.wait_ge(kv_heads_ready, b + 1)
                pe.wait_ge(q_ready, KC * (b + 1))
                for c in range(KC):
                    pe.matmul(y_bank[c][:, :], kv_heads[:, c, :], q_fm[:, c, :], start=True,
                              stop=True).then_inc(attended, 1)

            def route(b):
                pe.wait_ge(x1t_lo_ready, KC * (b + 1))
                for t in range(TT):
                    dst = t_bank[1][:, t * E:(t + 1) * E]
                    for c in range(KC):
                        hi, lo = xT_hi[:, c, b, t * P:(t + 1) * P], xT_lo[:, c, b, t * P:(t + 1) * P]
                        pe.matmul(dst, hi, gwT_hi[:, c, :], start=c == 0, stop=False)
                        pe.matmul(dst, hi, gwT_lo[:, c, :], start=False, stop=False)
                        pe.matmul(dst, lo, gwT_hi[:, c, :], start=False, stop=False)
                        last = pe.matmul(dst, lo, gwT_lo[:, c, :], start=False, stop=c == KC - 1)
                last.then_inc(logits_ready, 1)

            def transpose_c(b):
                pe.wait_ge(c_ready, b + 1)
                for t in range(TT):
                    last = pe.transpose(t_bank[0][0:E, t * P:(t + 1) * P], c_tok[:, t, :], ident[:, :])
                last.then_inc(c_transposed, 1)

            def batch(b, prev, prev2, nxt):
                pe.wait_ge(xt_lo_ready, KC * (b + 1))
                project_kv(b, 0)
                project_kv(b, 1)
                if prev:
                    project_out(b - 1)
                if prev2:
                    pe.wait_ge(x1t_lo_ready, KC * (b - 2) + 1)
                    transpose_c(b - 2)
                project_kv(b, 2)
                project_kv(b, 3)
                if nxt:
                    pe.wait_ge(x_loaded, 16 * (b + 2))
                if prev2:
                    pe.wait_ge(ct_copied, b - 1)
                    pe.wait_ge(gating_step, GATING_STEPS * (b - 2) + 2)
                if nxt:
                    transpose_x(x_in, x_transposed)
                if prev:
                    pe.wait_ge(gate_ready, KC * b)
                project_features(b, 0, 2 * D, q_projected)
                project_features(b, 1, 2 * D, q_projected)
                if nxt:
                    pe.wait_ge(xt_lo_ready, KC * (b + 2))
                if prev:
                    pe.wait_ge(x1_ready, b)
                    transpose_x(x1_sb, x1_transposed)
                pe.wait_ge(q_min_ready, KC * b + 1)
                pe.wait_ge(q_relu_ready, KC * b + 1)
                project_features(b, 0, 3 * D, g_projected)
                sum_kv(b)
                pe.wait_ge(q_min_ready, KC * b + 2)
                pe.wait_ge(q_relu_ready, KC * b + 2)
                project_features(b, 1, 3 * D, g_projected)
                if prev:
                    route(b - 1)
                    pe.wait_ge(residual_ready, 2 * b)
                attend(b)

            pe.wait_ge(const_ready, 6)
            pe.wait_ge(x_loaded, 16)
            transpose_x(x_in, x_transposed)
            pe.wait_ge(small_loaded, 16 * 7)
            for c in range(KC):
                last = pe.transpose(y_bank[0][:, c * E:(c + 1) * E], gw_sb[:, c * P:(c + 1) * P], ident[0:E, 0:E])
            last.then_inc(gw_transposed, 1)
            pe.wait_ge(wa_lo_ready, 2)
            pe.wait_ge(gw_lo_ready, 1)
            batch(0, False, False, True)
            batch(1, True, False, True)
            with pe.Fori(2, NB - 1) as b:
                batch(b, True, True, True)
            batch(NB - 1, True, True, False)

            def up(n, j, par, fresh=False):
                if not fresh:
                    pe.wait_ge(a_ready, NCH * n + j - 1)
                for k, done in enumerate((h1_ready, h3_ready)):
                    for c in range(KC):
                        cols = slice((k * KC + c) * INTER, (k * KC + c + 1) * INTER)
                        last = product(h_banks[par][k][:, :], we_hi[:, j, cols], we_lo[:, j, cols],
                                       xT_hi[:, c, n, :], xT_lo[:, c, n, :], c == 0, c == KC - 1)
                    last.then_inc(done, 1)

            def down(n, j, par, start=False, stop=False):
                pe.wait_ge(a_lo_ready, NCH * n + j + 1)
                for c in range(KC):
                    cols = slice(W13 + c * P, W13 + (c + 1) * P)
                    last = product(y_bank[c][:, :], we_hi[:, j, cols], we_lo[:, j, cols],
                                   a_hi[par][:, :], a_lo[par][:, :], start, stop)
                last.then_inc(down_done, 1)

            def transpose_y(n):
                pe.wait_ge(y0_copied, n + 1)
                pe.wait_ge(y1_copied, n + 1)
                for h in range(2):
                    for t in range(2 * h, 2 * h + 2):
                        for c in range(KC):
                            last = pe.transpose(t_bank[h][:, (t % 2) * D + c * P:(t % 2) * D + (c + 1) * P],
                                                yT[:, c, t * P:(t + 1) * P], ident[:, :])
                    last.then_inc(y_transposed, 1)

            def block_of(n, first, second=False):
                if first:
                    pe.wait_ge(we_lo_ready, 2)
                    pe.wait_ge(kv_biased, TT * NB)
                    pe.wait_ge(kv_heads_ready, NB)
                up(n, 0, 0, fresh=first)
                if first:
                    project_out(NB - 1)
                    pe.wait_ge(gate_ready, KC * NB)
                else:
                    down(n - 1, NCH - 1, 1, stop=True)
                    if second:
                        pe.wait_ge(x1t_lo_ready, KC * NB - 1)
                        transpose_c(NB - 1)
                up(n, 1, 1, fresh=first)
                if first:
                    pe.wait_ge(x1t_lo_ready, KC * (NB - 2) + 1)
                    transpose_c(NB - 2)
                    pe.wait_ge(residual_ready, 2 * NB)
                else:
                    if second:
                        pe.wait_ge(ct_copied, NB)
                        pe.wait_ge(gating_step, GATING_STEPS * (NB - 1) + 2)
                    else:
                        pe.wait_ge(residual_ready, 2 * (NB + n - 1))
                    transpose_y(n - 1)
                down(n, 0, 0, start=True)
                if first:
                    pe.wait_ge(x1_ready, NB)
                    pe.wait_ge(ct_copied, NB - 1)
                    pe.wait_ge(gating_step, GATING_STEPS * (NB - 2) + 2)
                    transpose_x(x1_sb, x1_transposed)
                    pe.wait_ge(we_lo_ready, PAIRS)
                with pe.Fori(0, QUADS) as q:
                    for r in range(RING):
                        j = SHARED + RING * q + r
                        up(n, j, r % 2)
                        down(n, j - 1, (r + 1) % 2)

            block_of(0, True)
            route(NB - 1)
            block_of(1, False, second=True)
            with pe.Fori(2, NB) as n:
                block_of(n, False)
            down(NB - 1, NCH - 1, 1, stop=True)
            pe.wait_ge(residual_ready, 2 * (2 * NB - 1))
            transpose_y(NB - 1)


_INS = ["L0_attn_x", "L0_attn_Wq", "L0_attn_bq", "L0_attn_Wk", "L0_attn_bk", "L0_attn_Wv", "L0_attn_bv",
        "L0_attn_Wg", "L0_attn_bg", "L0_attn_Wo", "L0_attn_bo", "L0_ffn_gate_w", "L0_ffn_w1", "L0_ffn_w2",
        "L0_ffn_w3", "L0_ffn_ws1", "L0_ffn_ws2", "L0_ffn_ws3"]


def kernel(**inputs):
    import numpy as _np
    import concourse.bacc as _bacc
    from concourse.bass_utils import run_bass_kernel_spmd as _run

    nc = _bacc.Bacc("TRN2", target_bir_lowering=False, num_devices=1)
    arrays, args = {}, []
    for name in _INS:
        a = _np.ascontiguousarray(inputs[name])
        arrays[f"in_{name}"] = a
        args.append(nc.dram_tensor(f"in_{name}", a.shape, mybir.dt.from_np(a.dtype), kind="ExternalInput").ap())
    shape = arrays["in_L0_attn_x"].shape
    args.append(nc.dram_tensor("out_0", shape, F32, kind="ExternalOutput").ap())
    attention_and_experts(nc, *args)
    r = _run(nc, [arrays], core_ids=[0])
    return r.results[0]["out_0"]
```

```python
from contextlib import ExitStack

import concourse.bass as bass
from concourse import mybir

F32 = mybir.dt.float32
HI = mybir.dt.float16
LO = mybir.dt.bfloat16
U32 = mybir.dt.uint32
I32 = mybir.dt.int32
ALU = mybir.AluOpType
ACT = mybir.ActivationFunctionType
AX_X = mybir.AxisListType.X

P = 128
PLAN_STEPS = 12
LN_EPS = 1e-5
HDIM = 16
GROUPS = 4
TOP_GROUPS = 2
TOP_K = 4
TAKEN = -1.0
FILLER = -2.0

GATING_STEPS = 15


def attention_and_experts(nc: bass.Bass, x, Wq, bq, Wk, bk, Wv, bv, Wg, bg, Wo, bo,
                          gate_w, w1, w2, w3, ws1, ws2, ws3, plan_consts, out):
    NB, S, D = x.shape
    KC = D // P
    TT = S // P
    E, _, INTER = w1.shape
    SHARED = ws1.shape[1] // INTER
    NCH = SHARED + E
    PAIRS = NCH // 2
    WAVES = 2
    WB = NB // WAVES
    WT = WB * TT
    NPAIR = WT * TOP_K // 2 + E
    PAIR = 2 * P
    SLOTS = NPAIR * PAIR
    MOST = WT // 2
    RING = 4
    GROUPS_OF_PAIRS = NPAIR // RING
    FILL_ROWS = 512
    FILLS = SLOTS // FILL_ROWS
    FILLS_PER_BATCH = 12
    assert (P, KC, TT, E, INTER, SHARED) == (128, 2, 4, 16, 128, 2) and NPAIR == RING * GROUPS_OF_PAIRS
    assert NB == 8 and WAVES == 2 and PAIRS == 9 and S == 512 and GROUPS_OF_PAIRS >= 2 * WB + 2
    assert WAVES * FILLS == 4 * FILLS_PER_BATCH and SLOTS == FILLS * FILL_ROWS
    W13 = 2 * KC * INTER
    WCOLS = W13 + D
    EG = E // GROUPS

    xs_dram = [nc.dram_tensor(f"expert_in{w}", (SLOTS, D), F32, kind="Internal").ap() for w in range(WAVES)]
    ys_dram = [nc.dram_tensor(f"expert_out{w}", (SLOTS, D), F32, kind="Internal").ap() for w in range(WAVES)]

    with ExitStack() as ctx:
        def sb(name, shape, dt=F32):
            return ctx.enter_context(nc.sbuf_tensor(name, shape, dt))

        def bank(name):
            return ctx.enter_context(nc.psum_tensor(name, [P, 512], F32))

        def sem(name):
            return ctx.enter_context(nc.semaphore(name))

        x_all = sb("x_all", [P, NB, TT, D])
        x_in = sb("x_in", [P, TT, D])
        x1_sb = sb("x1_sb", [P, TT, D])
        xT_hi = sb("xT_hi", [P, KC, NB, S], HI)
        xT_lo = sb("xT_lo", [P, KC, NB, S], LO)
        wa_hi = sb("wa_hi", [P, KC, 4 * D], HI)
        wa_lo = sb("wa_lo", [P, KC, 4 * D], LO)
        wo_sb = sb("wo_sb", [P, KC, D])
        we_hi = sb("we_hi", [P, NCH, WCOLS], HI)
        we_lo = sb("we_lo", [P, NCH, WCOLS], LO)
        stage = sb("stage", [P, 2, WCOLS])
        wa_stage = sb("wa_stage", [P, KC, 4 * D])
        wa_flat = wa_stage[:, :, :].rearrange("p c n -> p (c n)")
        zeros = wa_flat[:, 0:FILL_ROWS * D // P]
        ident = sb("ident", [P, P])
        head_mask = sb("head_mask", [P, KC, P])
        earlier = sb("earlier", [P, TT, GROUPS, GROUPS])
        minus_half = sb("minus_half", [P, TT])
        eps = sb("eps", [P, TT])
        b_kv = sb("b_kv", [P, 2 * D])
        b_o = sb("b_o", [P, D])
        b_q = sb("b_q", [P, KC])
        b_g = sb("b_g", [P, KC])
        gw_sb = sb("gw_sb", [E, D])
        gwT_hi = sb("gwT_hi", [P, KC, E], HI)
        gwT_lo = sb("gwT_lo", [P, KC, E], LO)
        kv = sb("kv", [P, TT, 2 * D])
        k_min = sb("k_min", [P, TT, D])
        q_min = sb("q_min", [P, KC, S])
        q_fm = sb("q_fm", [P, KC, S])
        gate = sb("gate", [P, KC, S])
        gated = sb("gated", [P, KC, S])
        kv_heads = sb("kv_heads", [P, KC, P])
        wait_pad = sb("wait_pad", [P, 1])
        bn = sb("bn", [P, TT, 6])
        mv = sb("mv", [P, TT, 2])
        var_eps = sb("var_eps", [P, TT])
        rstd = sb("rstd", [P, TT])
        r_max = sb("r_max", [P, TT])
        r_sub = sb("r_sub", [P, TT, E])
        r_exp = sb("r_exp", [P, TT, E])
        r_sum = sb("r_sum", [P, TT])
        r_inv = sb("r_inv", [P, TT])
        score = sb("score", [P, TT, E])
        g_max = sb("g_max", [P, TT, GROUPS])
        g_gt = sb("g_gt", [P, TT, GROUPS, GROUPS])
        g_eq = sb("g_eq", [P, TT, GROUPS, GROUPS])
        g_rank = sb("g_rank", [P, TT, GROUPS])
        g_sel = sb("g_sel", [P, TT, GROUPS])
        masked = sb("masked", [P, TT, E + 8 - TOP_K])
        top8 = sb("top8", [P, TT, 8])
        marked = sb("marked", [P, TT, E + 8 - TOP_K])
        sel_all = sb("sel_all", [P, NB, TT, E], HI)
        c_all = sb("c_all", [P, NB, TT, E])
        plan_sb = sb("plan_sb", [P, P + E * E + MOST + NPAIR])
        before_f = plan_sb[:, 0:P]
        earlier_e = plan_sb[:, P:P + E * E].rearrange("p (e f) -> p e f", e=E)
        starts = plan_sb[:, P + E * E:P + E * E + MOST]
        pair_no = plan_sb[:, P + E * E + MOST:]
        before = sb("before", [P, P], HI)
        ones = sb("ones", [P, P], HI)
        prefix = sb("prefix", [P, (WT + 1) * E])
        work = stage[:, :, :].rearrange("p s n -> p (s n)")
        n_pairs = sb("n_pairs", [P, E])
        first_pair = sb("first_pair", [P, E])
        pairs_end = sb("pairs_end", [P, E])
        first_slot = sb("first_slot", [P, E])
        slot_of = sb("slot_of", [P, WT, E])
        slot8 = sb("slot8", [P, WT, 8])
        slots = [sb(f"slots{w}", [P, WT, TOP_K], U32) for w in range(WAVES)]
        c_of_slot = [sb(f"c_of_slot{w}", [P, WT, TOP_K]) for w in range(WAVES)]
        pair_expert_f = sb("pair_expert_f", [1, NPAIR])
        pair_chunk = sb("pair_chunk", [1, WAVES * NPAIR, 1], I32)
        a_hi = [sb(f"a_hi{i}", [P, S], HI) for i in range(2)]
        a_lo = [sb(f"a_lo{i}", [P, S], LO) for i in range(2)]
        xsT_hi = [sb(f"xsT_hi{i}", [P, KC, 2 * P], HI) for i in range(2)]
        xsT_lo = [sb(f"xsT_lo{i}", [P, KC, 2 * P], LO) for i in range(2)]
        aT_hi = [sb(f"aT_hi{i}", [P, 2 * P], HI) for i in range(2)]
        aT_lo = [sb(f"aT_lo{i}", [P, 2 * P], LO) for i in range(2)]
        xs = [kv[:, r, :].rearrange("p (t d) -> p t d", t=2) for r in range(RING)]
        flat = "p c n -> p (c n)"
        ys = [buf[:, :, :].rearrange(flat)[:, i * 2 * D:(i + 1) * 2 * D].rearrange("p (t d) -> p t d", t=2)
              for buf in (k_min, q_min) for i in range(2)]
        y_got = [buf[:, :, :].rearrange(flat).rearrange("p (k d) -> p k d", k=TOP_K) for buf in (q_fm, gate)]
        y_got += [wa_flat[:, i * TOP_K * D:(i + 1) * TOP_K * D].rearrange("p (k d) -> p k d", k=TOP_K)
                  for i in range(2)]
        o_sb = gated[:, :, :].rearrange(flat).rearrange("p (t d) -> p t d", t=TT)
        s_act = x_in[:, :, :].rearrange(flat)[:, 0:S]
        a_act = x_in[:, :, :].rearrange(flat)[:, S:2 * S]
        s_pair, a_pair = x1_sb[:, 0, :], x1_sb[:, 1, :]

        h_banks = [[bank("h1_even"), bank("h3_even")], [bank("h1_odd"), bank("h3_odd")]]
        kv_bank = h_banks[0]
        qg_bank = h_banks[1]
        y_bank = [bank("y0"), bank("y1")]
        t_bank = [bank("t0"), bank("t1")]

        x_loaded, wa_loaded, small_loaded = sem("x_loaded"), sem("wa_loaded"), sem("small_loaded")
        stage_loaded, out_stored = sem("stage_loaded"), sem("out_stored")
        zeros_ready = sem("zeros_ready")
        zero_filled = [sem(f"zero_filled{w}") for w in range(WAVES)]
        dispatched = [sem(f"dispatched{b}") for b in range(NB)]
        xs_loaded = [sem(f"xs_loaded{r}") for r in range(RING)]
        ys_stored = [sem(f"ys_stored{r}") for r in range(RING)]
        y_gathered = [sem(f"y_gathered{i}") for i in range(RING)]
        const_step, const_ready = sem("const_step"), sem("const_ready")
        wa_hi_ready, wa_lo_ready = sem("wa_hi_ready"), sem("wa_lo_ready")
        gw_transposed, gw_hi_ready, gw_lo_ready = sem("gw_transposed"), sem("gw_hi_ready"), sem("gw_lo_ready")
        we_hi_ready, we_lo_ready = sem("we_hi_ready"), sem("we_lo_ready")
        x_transposed, xt_hi_ready, xt_lo_ready = sem("x_transposed"), sem("xt_hi_ready"), sem("xt_lo_ready")
        kv_projected, kv_biased = sem("kv_projected"), sem("kv_biased")
        k_min_ready, k_exp_ready, k_ready = sem("k_min_ready"), sem("k_exp_ready"), sem("k_ready")
        q_projected, q_min_ready, q_relu_ready = sem("q_projected"), sem("q_min_ready"), sem("q_relu_ready")
        q_exp_ready, q_ready = sem("q_exp_ready"), sem("q_ready")
        g_projected, gate_ready = sem("g_projected"), sem("gate_ready")
        kv_summed, kv_heads_ready = sem("kv_summed"), sem("kv_heads_ready")
        attended, gated_ready = sem("attended"), sem("gated_ready")
        wo_projected, x_biased, residual_ready = sem("wo_projected"), sem("x_biased"), sem("residual_ready")
        bn_ready, mv_ready, var_eps_ready, rstd_ready = sem("bn_ready"), sem("mv_ready"), sem("var_eps_ready"), sem("rstd_ready")
        x1_ready, x1_transposed, x1_kept = sem("x1_ready"), sem("x1_transposed"), sem("x1_kept")
        x1t_hi_ready, x1t_lo_ready = sem("x1t_hi_ready"), sem("x1t_lo_ready")
        logits_ready, gating_step, r_exp_ready = sem("logits_ready"), sem("gating_step"), sem("r_exp_ready")
        c_ready, counted, plan_copied, plan_step = sem("c_ready"), sem("counted"), sem("plan_copied"), sem("plan_step")
        count_consts_ready, slots_ready = sem("count_consts_ready"), sem("slots_ready")
        experts_ready, c_of_slot_ready, weight_step = sem("experts_ready"), sem("c_of_slot_ready"), sem("weight_step")
        xs_transposed, xst_hi_ready, xst_lo_ready = sem("xs_transposed"), sem("xst_hi_ready"), sem("xst_lo_ready")
        h_ready, pair_silu_ready, pair_a_ready = sem("h_ready"), sem("pair_silu_ready"), sem("pair_a_ready")
        at_hi_ready, at_lo_ready = sem("at_hi_ready"), sem("at_lo_ready")
        ys_ready, ys_copied, combined = sem("ys_ready"), sem("ys_copied"), sem("combined")
        h1_ready, h3_ready, silu_ready = sem("h1_ready"), sem("h3_ready"), sem("silu_ready")
        a_ready, a_hi_ready, a_lo_ready = sem("a_ready"), sem("a_hi_ready"), sem("a_lo_ready")
        down_done, shared_added = sem("down_done"), sem("shared_added")
        out_ready = sem("out_ready")

        def stage_sources(m):
            if isinstance(m, int) and m == 0:
                return [(ws1[:, s * INTER:(s + 1) * INTER], ws3[:, s * INTER:(s + 1) * INTER],
                         ws2[s * INTER:(s + 1) * INTER, :]) for s in range(SHARED)]
            return [(w1[2 * m - 2 + s], w3[2 * m - 2 + s], w2[2 * m - 2 + s]) for s in range(2)]

        def late(i, n):
            return not isinstance(i, int) or i >= n

        block = ctx.enter_context(nc.Block())

        @block.sync
        def _(sp):
            def load_x(b):
                sp.dma_start(x_in[:, :, :], x[b].rearrange("(t p) d -> p t d", p=P)).then_inc(x_loaded, 16)

            def load_stage(m):
                for s, (a1, a3, a2) in enumerate(stage_sources(m)):
                    for k, src in enumerate((a1, a3)):
                        dst = stage[:, s, 0:W13].rearrange("p (c k i) -> p c k i", c=KC, k=2)[:, :, k, :]
                        sp.dma_start(dst,
                                     src.rearrange("(c p) i -> p c i", p=P)).then_inc(stage_loaded, 16)
                    sp.dma_start(stage[:, s, W13:], a2).then_inc(stage_loaded, 16)

            load_x(0)
            for k, w in enumerate((Wk, Wv, Wq, Wg)):
                sp.dma_start(wa_stage[:, :, k * D:(k + 1) * D],
                             w.rearrange("(c p) n -> p c n", p=P)).then_inc(wa_loaded, 16)
            sp.dma_start(b_kv[:, 0:D], bk.partition_broadcast(P)).then_inc(small_loaded, 16)
            sp.dma_start(b_kv[:, D:], bv.partition_broadcast(P)).then_inc(small_loaded, 16)
            sp.dma_start(b_o[:, :], bo.partition_broadcast(P)).then_inc(small_loaded, 16)
            sp.dma_start(wo_sb[:, :, :], Wo.rearrange("(c p) n -> p c n", p=P)).then_inc(small_loaded, 16)
            sp.dma_start(gw_sb[:, :], gate_w).then_inc(small_loaded, 16)
            sp.dma_start(plan_sb[:, :], plan_consts).then_inc(small_loaded, 16)
            load_stage(0)

            xs_fill = [x_.rearrange("(n p r) d -> n p (r d)", p=P, r=FILL_ROWS // P) for x_ in xs_dram]
            xs_pairs = [x_.rearrange("(g t p) d -> g p t d", t=2, p=P) for x_ in xs_dram]
            ys_pairs = [y_.rearrange("(g t p) d -> g p t d", t=2, p=P) for y_ in ys_dram]

            def fill(i):
                w = i // FILLS
                sp.dma_start(xs_fill[w][i % FILLS], zeros).then_inc(zero_filled[w], 16)

            def next_x(b):
                sp.wait_ge(x_biased, b)
                load_x(b)

            def next_stage(m):
                sp.wait_ge(we_lo_ready, m)
                load_stage(m)

            next_x(1)
            sp.wait_ge(zeros_ready, 1)
            next_stage(1)
            next_x(2)
            for b in range(1, 5):
                next_stage(2 * b)
                next_x(b + 2)
                for i in range(FILLS_PER_BATCH):
                    fill(FILLS_PER_BATCH * (b - 1) + i)
                if 2 * b + 1 < PAIRS:
                    next_stage(2 * b + 1)
            next_x(NB - 1)

            def load_xs(w, p, r, first=False):
                if not first:
                    sp.wait_ge(xs_transposed, NPAIR * w + p - RING + 1)
                sp.dma_start(xs[r][:, :, :], xs_pairs[w][p]).then_inc(xs_loaded[r], 16)

            def store_ys(w, p, r):
                sp.wait_ge(ys_copied, NPAIR * w + p + 1)
                sp.dma_start(ys_pairs[w][p], ys[r][:, :, :]).then_inc(ys_stored[r], 16)

            def store_out(b):
                sp.wait_ge(out_ready, b + 1)
                sp.dma_start(out[b].rearrange("(t p) d -> p t d", p=P), o_sb[:, :, :]).then_inc(out_stored, 16)

            def group(w, q):
                for r in range(RING):
                    load_xs(w, RING * (q + 1) + r, r)
                    store_ys(w, RING * q + r, r)

            last = GROUPS_OF_PAIRS - 1
            for b in range(WB):
                sp.wait_ge(dispatched[b], 16 * TT * TOP_K)
            sp.wait_ge(kv_summed, NB)
            for r in range(RING):
                load_xs(0, r, r, first=True)
            with sp.Fori(0, last) as q:
                group(0, q)
            for b in range(WB, NB):
                sp.wait_ge(dispatched[b], 16 * TT * TOP_K)
            for r in range(RING):
                load_xs(1, r, r)
                store_ys(0, RING * last + r, r)
            with sp.Fori(0, 4) as q:
                group(1, q)
            with sp.Fori(1, WB - 1) as b:
                store_out(b - 1)
                group(1, 2 * b + 2)
                group(1, 2 * b + 3)
            store_out(WB - 2)
            with sp.Fori(2 * WB, last) as q:
                group(1, q)
            for r in range(RING):
                store_ys(1, RING * last + r, r)
            with sp.Fori(WB - 1, NB) as b:
                store_out(b)
            sp.wait_ge(out_stored, 16 * NB)

        @block.gpsimd
        def _(pool):
            pool.memset(ident[:, :], 0.0).then_inc(const_step, 1)
            pool.memset(head_mask[:, :, :], 1.0).then_inc(const_step, 1)
            pool.memset(earlier[:, :, :, :], 1.0).then_inc(const_step, 1)
            pool.memset(minus_half[:, :], -0.5).then_inc(const_ready, 1)
            pool.memset(eps[:, :], LN_EPS).then_inc(const_ready, 1)
            pool.memset(masked[:, :, E:], FILLER).then_inc(const_ready, 1)
            pool.wait_ge(const_step, 3)
            pool.affine_select(out=ident[:, :], in_=ident[:, :], compare_op=ALU.not_equal, fill=1.0,
                               base=0, pattern=[[-1, P]], channel_multiplier=1).then_inc(const_ready, 1)
            pool.affine_select(out=earlier[:, :, :, :], in_=earlier[:, :, :, :], compare_op=ALU.is_ge, fill=0.0,
                               base=-1, pattern=[[0, TT], [1, GROUPS], [-1, GROUPS]],
                               channel_multiplier=0).then_inc(const_ready, 1)
            heads = head_mask[:, :, :].rearrange("p c (h e) -> p c h e", e=HDIM)
            pool.affine_select(out=heads, in_=heads, compare_op=ALU.is_ge, fill=0.0, base=0,
                               pattern=[[0, KC], [-HDIM, P // HDIM], [0, HDIM]],
                               channel_multiplier=1).then_inc(const_step, 1)
            pool.wait_ge(const_step, 4)
            pool.affine_select(out=heads, in_=heads, compare_op=ALU.is_ge, fill=0.0, base=HDIM - 1,
                               pattern=[[0, KC], [HDIM, P // HDIM], [0, HDIM]],
                               channel_multiplier=-1).then_inc(const_ready, 1)
            pool.wait_ge(const_ready, 6)
            pool.wait_ge(small_loaded, 16 * 8)

            def rstd_of(ln):
                pool.wait_ge(mv_ready, ln + 1)
                pool.tensor_tensor(var_eps[:, :], mv[:, :, 1], eps[:, :], ALU.add).then_inc(var_eps_ready, 1)
                pool.wait_ge(var_eps_ready, ln + 1)
                pool.tensor_tensor(rstd[:, :], var_eps[:, :], minus_half[:, :], ALU.pow).then_inc(rstd_ready, 1)

            def split_lo(m):
                pool.wait_ge(we_hi_ready, m + 1)
                for s in range(2):
                    c = 2 * m + s
                    last = pool.tensor_tensor(we_lo[:, c, :], stage[:, s, :], we_hi[:, c, :], ALU.subtract)
                last.then_inc(we_lo_ready, 1)

            def batch(b, has_prev, pairs, before_q=(), after_q=()):
                if has_prev:
                    rstd_of(b - 1)
                if pairs:
                    split_lo(pairs[0])
                dispatch(before_q)
                for c in range(KC):
                    pool.wait_ge(q_exp_ready, KC * b + c + 1)
                    pool.tensor_tensor(q_fm[:, c, :], q_fm[:, c, :], q_min[:, c, :], ALU.add).then_inc(q_ready, 1)
                for m in pairs[1:]:
                    split_lo(m)
                dispatch(after_q)

            def dispatch(rows):
                for k, j in rows:
                    b, w = k // TT, k // WT
                    if k % WT == 0 and j == 0:
                        pool.wait_ge(slots_ready, w + 1)
                        pool.wait_ge(x1_kept, WB * (w + 1))
                        pool.wait_ge(zero_filled[w], 16 * FILLS)
                    pool.indirect_dma_start(xs_dram[w], bass.IndirectOffsetOnAxis(ap=slots[w][:, k % WT, j:j + 1], axis=0),
                                            x_all[:, b, k % TT, :], None).then_inc(dispatched[b], 16)

            def gather(k):
                w, i = k // WT, k % RING
                if k >= RING:
                    pool.wait_ge(combined, TOP_K * (k - RING + 1))
                for j in range(TOP_K):
                    pool.indirect_dma_start(y_got[i][:, j, :], None, ys_dram[w],
                                            bass.IndirectOffsetOnAxis(ap=slots[w][:, k % WT, j:j + 1], axis=0)
                                            ).then_inc(y_gathered[i], 16)

            rows = [(k, j) for k in range(NB * TT) for j in range(TOP_K)]
            batch(0, False, [0])
            with pool.Fori(1, 5) as b:
                batch(b, True, [2 * b - 1, 2 * b])
            batch(5, True, [])
            batch(6, True, [], (), rows[0:8])
            batch(7, True, [], rows[8:14], rows[14:20])
            dispatch(rows[20:23])
            rstd_of(NB - 1)
            dispatch(rows[23:])
            pool.wait_ge(attended, KC * NB)
            pool.wait_ge(gated_ready, KC * NB)
            for w in range(WAVES):
                for r in range(RING):
                    pool.wait_ge(ys_stored[r], 16 * GROUPS_OF_PAIRS * (w + 1))
                for b in range(WB * w, WB * (w + 1)):
                    gather(TT * b)
                    gather(TT * b + 1)
                    if b > WB * w:
                        rstd_of(NB + b - 1)
                    gather(TT * b + 2)
                    gather(TT * b + 3)
                rstd_of(NB + WB * (w + 1) - 1)

        @block.scalar
        def _(act):
            act.dma_start(b_q[:, :], bq.rearrange("(c p) -> p c", p=P), allow_slow_non_contiguous=True).then_inc(small_loaded, 16)
            act.dma_start(b_g[:, :], bg.rearrange("(c p) -> p c", p=P), allow_slow_non_contiguous=True).then_inc(small_loaded, 16)

            def xt_hi(b):
                for c in range(KC):
                    act.wait_ge(x_transposed, KC * b + c + 1)
                    act.activation(xT_hi[:, c, b, :], t_bank[c][:, :], ACT.Copy).then_inc(xt_hi_ready, 1)

            def x1t_hi(b):
                for c in range(KC):
                    act.wait_ge(x1_transposed, KC * b + c + 1)
                    act.activation(xT_hi[:, c, b, :], t_bank[c][:, :], ACT.Copy).then_inc(x1t_hi_ready, 1)

            def keep_x1(b):
                act.wait_ge(x1_ready, b + 1)
                act.activation(x_all[:, b, :, :], x1_sb[:, :, :], ACT.Copy).then_inc(x1_kept, 1)

            def split_hi(m):
                act.wait_ge(stage_loaded, 16 * 6 * (m + 1))
                act.activation(we_hi[:, 2 * m, :], stage[:, 0, :], ACT.Copy)
                act.activation(we_hi[:, 2 * m + 1, :], stage[:, 1, :], ACT.Copy).then_inc(we_hi_ready, 1)

            def routing_exp(b):
                act.wait_ge(gating_step, GATING_STEPS * b + 2)
                act.activation(r_exp[:, :, :], r_sub[:, :, :], ACT.Exp).then_inc(r_exp_ready, 1)

            def batch(b, prev, prev2, nxt, pairs=()):
                if prev2:
                    routing_exp(b - 2)
                if pairs:
                    split_hi(pairs[0])
                if nxt:
                    xt_hi(b + 1)
                act.wait_ge(small_loaded, 16 * 8)

                def q_relu(c):
                    act.wait_ge(q_projected, KC * b + c + 1)
                    if prev:
                        act.wait_ge(attended, KC * b)
                    act.activation(q_fm[:, c, :], qg_bank[c][:, :], ACT.Relu, bias=b_q[:, c:c + 1]).then_inc(q_relu_ready, 1)

                def q_expo(c):
                    act.wait_ge(q_min_ready, KC * b + c + 1)
                    act.wait_ge(q_relu_ready, KC * b + c + 1)
                    act.activation(q_min[:, c, :], q_min[:, c, :], ACT.Exp).then_inc(q_exp_ready, 1)

                q_relu(0)
                act.wait_ge(k_min_ready, b + 1)
                act.activation(k_min[:, :, :], k_min[:, :, :], ACT.Exp).then_inc(k_exp_ready, 1)
                q_expo(0)
                q_relu(1)
                if prev:
                    x1t_hi(b - 1)
                q_expo(1)
                if prev:
                    keep_x1(b - 1)
                for c in range(KC):
                    act.wait_ge(g_projected, KC * b + c + 1)
                    if prev:
                        act.wait_ge(gated_ready, KC * b)
                    act.activation(gate[:, c, :], qg_bank[c][:, :], ACT.Sigmoid, bias=b_g[:, c:c + 1]).then_inc(gate_ready, 1)
                for m in pairs[1:]:
                    split_hi(m)

            xt_hi(0)
            act.wait_ge(wa_loaded, 16 * 4)
            act.activation(wa_hi[:, :, 0:2 * D], wa_stage[:, :, 0:2 * D], ACT.Copy).then_inc(wa_hi_ready, 1)
            act.activation(wa_hi[:, :, 2 * D:], wa_stage[:, :, 2 * D:], ACT.Copy).then_inc(wa_hi_ready, 1)
            act.wait_ge(gw_transposed, 1)
            act.activation(gwT_hi[:, :, :], y_bank[0][:, 0:KC * E].rearrange("p (c e) -> p c e", c=KC),
                           ACT.Copy).then_inc(gw_hi_ready, 1)
            batch(0, False, False, True, [0])
            batch(1, True, False, True, [1, 2])
            with act.Fori(2, 5) as b:
                batch(b, True, True, True, [2 * b - 1, 2 * b])
            with act.Fori(5, NB - 1) as b:
                batch(b, True, True, True)
            batch(NB - 1, True, True, False)
            routing_exp(NB - 2)

            act.wait_ge(x_biased, NB)

            def shared_block(n):
                for par in range(SHARED):
                    act.wait_ge(h1_ready, SHARED * n + par + 1)
                    if late(n, 1) or par:
                        act.wait_ge(a_ready, SHARED * n + par)
                    act.activation(s_act[:, :], h_banks[par][0][:, :], ACT.Silu).then_inc(silu_ready, 1)
                    act.wait_ge(a_ready, SHARED * n + par + 1)
                    if late(n, 1):
                        act.wait_ge(down_done, n)
                    act.activation(a_hi[par][:, :], a_act[:, :], ACT.Copy).then_inc(a_hi_ready, 1)
                    if isinstance(n, int) and n == 0 and par == 1:
                        x1t_hi(NB - 1)
                        keep_x1(NB - 1)

            shared_block(0)
            shared_block(1)
            routing_exp(NB - 1)
            with act.Fori(2, WB) as n:
                shared_block(n)

            def xst_hi(g, r):
                act.wait_ge(xs_transposed, g + 1)
                if late(g, 2):
                    act.wait_ge(h_ready, g - 1)
                act.activation(xsT_hi[r % 2][:, :, :], t_bank[r % 2][:, :].rearrange("p (c n) -> p c n", c=KC),
                               ACT.Copy).then_inc(xst_hi_ready, 1)

            def ys_copy(g, r, group):
                act.wait_ge(ys_ready, g + 1)
                if late(group, 1):
                    act.wait_ge(ys_stored[r], 16 * group)
                act.activation(ys[r][:, :, :], y_bank[r % 2][:, :].rearrange("p (t d) -> p t d", t=2),
                               ACT.Copy).then_inc(ys_copied, 1)

            def pair(g, r, ahead=True):
                if ahead:
                    xst_hi(g + 1, r + 1)
                act.wait_ge(h_ready, g + 1)
                if late(g, 1):
                    act.wait_ge(pair_a_ready, g)
                act.activation(s_pair[:, :], h_banks[r % 2][0][:, 0:2 * P], ACT.Silu).then_inc(pair_silu_ready, 1)
                act.wait_ge(pair_a_ready, g + 1)
                if late(g, 2):
                    act.wait_ge(ys_ready, g - 1)
                act.activation(aT_hi[r % 2][:, :], a_pair[:, :], ACT.Copy).then_inc(at_hi_ready, 1)

            def group(q, last=False):
                for r in range(RING):
                    pair(RING * q + r, r, not (last and r == RING - 1))
                    if r > 0:
                        ys_copy(RING * q + r - 1, r - 1, q)
                    elif late(q, 1):
                        ys_copy(RING * q - 1, RING - 1, q - 1)

            all_groups = WAVES * GROUPS_OF_PAIRS
            act.wait_ge(k_ready, NB)
            act.wait_ge(q_ready, KC * NB)
            xst_hi(0, 0)
            group(0)
            group(1)
            with act.Fori(2, all_groups - 1) as q:
                group(q)
            group(all_groups - 1, last=True)
            ys_copy(RING * all_groups - 1, RING - 1, all_groups - 1)
            with act.Fori(WB, NB) as n:
                shared_block(n)

        @block.vector
        def _(dve):
            def xt_lo(b):
                for c in range(KC):
                    dve.wait_ge(xt_hi_ready, KC * b + c + 1)
                    dve.tensor_tensor(xT_lo[:, c, b, :], t_bank[c][:, :], xT_hi[:, c, b, :],
                                      ALU.subtract).then_inc(xt_lo_ready, 1)

            def x1t_lo(b):
                for c in range(KC):
                    dve.wait_ge(x1t_hi_ready, KC * b + c + 1)
                    dve.tensor_tensor(xT_lo[:, c, b, :], t_bank[c][:, :], xT_hi[:, c, b, :],
                                      ALU.subtract).then_inc(x1t_lo_ready, 1)

            def kv_bias(b, t, prev):
                dve.wait_ge(kv_projected, TT * b + t + 1)
                if prev:
                    dve.wait_ge(kv_summed, b)
                dve.tensor_tensor(kv[:, t, :], kv_bank[t % 2][:, :], b_kv[:, :], ALU.add).then_inc(kv_biased, 1)

            def apply_gate(b, has_prev):
                for c in range(KC):
                    dve.wait_ge(attended, KC * b + c + 1)
                    dve.wait_ge(gate_ready, KC * b + c + 1)
                    if has_prev:
                        dve.wait_ge(wo_projected, 2 * b)
                    dve.tensor_tensor(gated[:, c, :], y_bank[c][:, :], gate[:, c, :], ALU.mult).then_inc(gated_ready, 1)

            def norm_stats(rows, ln):
                for t in range(TT):
                    last = dve.bn_stats(bn[:, t, :], rows(t))
                last.then_inc(bn_ready, 1)
                dve.wait_ge(bn_ready, ln + 1)
                dve.memset(wait_pad[:, :], 0.0)
                for t in range(TT):
                    last = dve.bn_aggr(mv[:, t, :], bn[:, t, :])
                last.then_inc(mv_ready, 1)

            def x1_rows(t):
                return x1_sb[:, t, :]

            def x_plus_bias(b):
                dve.wait_ge(x_transposed, KC * (b + 1))
                dve.tensor_tensor(x_all[:, b, :, :], x_in[:, :, :],
                                  b_o[:, :].unsqueeze(1).to_broadcast([P, TT, D]), ALU.add).then_inc(x_biased, 1)

            def normalize(rows, outs, ln, done):
                dve.wait_ge(rstd_ready, ln + 1)
                for t in range(TT):
                    last = dve.tensor_scalar(outs(t), rows(t), mv[:, t, 0:1], rstd[:, t:t + 1],
                                             ALU.subtract, ALU.mult)
                last.then_inc(done, 1)

            def residual(b, has_prev):
                dve.wait_ge(x_biased, b + 1)
                if has_prev:
                    dve.wait_ge(x1_transposed, KC * b)
                    dve.wait_ge(x1_kept, b)
                for h in range(2):
                    dve.wait_ge(wo_projected, 2 * b + h + 1)
                    dve.tensor_tensor(x1_sb[:, 2 * h:2 * h + 2, :],
                                      y_bank[h][:, :].rearrange("p (t d) -> p t d", t=2),
                                      x_all[:, b, 2 * h:2 * h + 2, :], ALU.add).then_inc(residual_ready, 1)
                dve.wait_ge(residual_ready, 2 * b + 2)
                norm_stats(x1_rows, b)

            def routing_head(b):
                at = GATING_STEPS * b
                logits = t_bank[1][:, 0:TT * E].rearrange("p (t e) -> p t e", t=TT)
                per_tile = [P, TT, E]
                dve.wait_ge(logits_ready, b + 1)
                dve.tensor_reduce(r_max[:, :], logits, AX_X, ALU.max).then_inc(gating_step, 1)
                dve.wait_ge(gating_step, at + 1)
                dve.tensor_tensor(r_sub[:, :, :], logits, r_max[:, :].unsqueeze(2).to_broadcast(per_tile),
                                  ALU.subtract).then_inc(gating_step, 1)

            def routing_tail(b):
                at = GATING_STEPS * b
                per_tile = [P, TT, E]
                dve.wait_ge(r_exp_ready, b + 1)
                dve.tensor_reduce(r_sum[:, :], r_exp[:, :, :], AX_X, ALU.add).then_inc(gating_step, 1)
                dve.wait_ge(gating_step, at + 3)
                dve.reciprocal(r_inv[:, :], r_sum[:, :]).then_inc(gating_step, 1)
                dve.wait_ge(gating_step, at + 4)
                dve.tensor_tensor(score[:, :, :], r_exp[:, :, :], r_inv[:, :].unsqueeze(2).to_broadcast(per_tile),
                                  ALU.mult).then_inc(gating_step, 1)
                dve.wait_ge(gating_step, at + 5)
                grouped = score[:, :, :].rearrange("p t (g e) -> p t g e", g=GROUPS)
                dve.tensor_reduce(g_max[:, :, :], grouped, AX_X, ALU.max).then_inc(gating_step, 1)
                dve.wait_ge(gating_step, at + 6)
                pairs = [P, TT, GROUPS, GROUPS]
                other = g_max[:, :, :].unsqueeze(2).to_broadcast(pairs)
                own = g_max[:, :, :].unsqueeze(3).to_broadcast(pairs)
                dve.tensor_tensor(g_gt[:, :, :, :], other, own, ALU.is_gt)
                dve.tensor_tensor(g_eq[:, :, :, :], other, own, ALU.is_equal).then_inc(gating_step, 1)
                dve.wait_ge(gating_step, at + 7)
                dve.tensor_tensor(g_eq[:, :, :, :], g_eq[:, :, :, :], earlier[:, :, :, :], ALU.mult).then_inc(gating_step, 1)
                dve.wait_ge(gating_step, at + 8)
                dve.tensor_tensor(g_gt[:, :, :, :], g_gt[:, :, :, :], g_eq[:, :, :, :], ALU.add).then_inc(gating_step, 1)
                dve.wait_ge(gating_step, at + 9)
                dve.tensor_reduce(g_rank[:, :, :], g_gt[:, :, :, :], AX_X, ALU.add).then_inc(gating_step, 1)
                dve.wait_ge(gating_step, at + 10)
                dve.tensor_scalar(g_sel[:, :, :], g_rank[:, :, :], float(TOP_GROUPS), None, ALU.is_lt).then_inc(gating_step, 1)
                dve.wait_ge(gating_step, at + 11)
                dve.tensor_tensor(masked[:, :, 0:E].rearrange("p t (g e) -> p t g e", g=GROUPS), grouped,
                                  g_sel[:, :, :].unsqueeze(3).to_broadcast([P, TT, GROUPS, EG]),
                                  ALU.mult).then_inc(gating_step, 1)
                dve.wait_ge(gating_step, at + 12)
                dve.memset(wait_pad[:, :], 0.0)
                for t in range(TT):
                    last = dve.max(top8[:, t, :], masked[:, t, 0:E])
                last.then_inc(gating_step, 1)
                dve.wait_ge(gating_step, at + 13)
                dve.memset(top8[:, :, TOP_K:], FILLER).then_inc(gating_step, 1)
                dve.wait_ge(gating_step, at + 14)
                dve.memset(wait_pad[:, :], 0.0)
                for t in range(TT):
                    last = dve.match_replace(marked[:, t, :], top8[:, t, :], masked[:, t, :], TAKEN)
                last.then_inc(gating_step, 1)
                dve.wait_ge(gating_step, at + 15)
                dve.tensor_scalar(sel_all[:, b, :, :], marked[:, :, 0:E], TAKEN, None, ALU.is_equal)
                dve.scalar_tensor_tensor(c_all[:, b, :, :], marked[:, :, 0:E], TAKEN, score[:, :, :],
                                         ALU.is_equal, ALU.mult).then_inc(c_ready, 1)

            def plan_copy(w):
                dve.wait_ge(counted, w + 1)
                dve.tensor_copy(prefix[:, :], t_bank[0][:, 0:(WT + 1) * E]).then_inc(plan_copied, 1)

            def plan_slots(w):
                at = PLAN_STEPS * w
                by_tile = [P, WT, E]
                total = prefix[:, WT * E:]
                over = work[:, 0:E * MOST].rearrange("p (e j) -> p e j", e=E)
                ahead = work[:, 0:E * E].rearrange("p (e f) -> p e f", e=E)
                dve.wait_ge(plan_copied, w + 1)
                dve.wait_ge(we_lo_ready, PAIRS)
                dve.tensor_tensor(over, total.unsqueeze(2).to_broadcast([P, E, MOST]),
                                  starts.unsqueeze(1).to_broadcast([P, E, MOST]), ALU.is_gt).then_inc(plan_step, 1)
                dve.wait_ge(plan_step, at + 1)
                dve.tensor_reduce(n_pairs[:, :], over, AX_X, ALU.add).then_inc(plan_step, 1)
                dve.wait_ge(plan_step, at + 2)
                dve.tensor_tensor(ahead, n_pairs[:, :].unsqueeze(1).to_broadcast([P, E, E]), earlier_e,
                                  ALU.mult).then_inc(plan_step, 1)
                dve.wait_ge(plan_step, at + 3)
                dve.tensor_reduce(first_pair[:, :], ahead, AX_X, ALU.add).then_inc(plan_step, 1)
                dve.wait_ge(plan_step, at + 4)
                dve.tensor_scalar(first_slot[:, :], first_pair[:, :], float(PAIR), 1.0, ALU.mult, ALU.add).then_inc(plan_step, 1)
                dve.wait_ge(plan_step, at + 5)
                dve.tensor_tensor(slot_of[:, :, :], prefix[:, 0:WT * E].rearrange("p (t e) -> p t e", t=WT),
                                  first_slot[:, :].unsqueeze(1).to_broadcast(by_tile), ALU.add).then_inc(plan_step, 1)
                dve.wait_ge(plan_step, at + 6)
                dve.tensor_tensor(slot_of[:, :, :], slot_of[:, :, :],
                                  sel_all[:, WB * w:WB * (w + 1), :, :].rearrange("p b t e -> p (b t) e"),
                                  ALU.mult).then_inc(plan_step, 1)
                dve.wait_ge(plan_step, at + 7)
                for t in range(WT):
                    last = dve.max(slot8[:, t, :], slot_of[:, t, :])
                last.then_inc(plan_step, 1)
                dve.wait_ge(plan_step, at + 8)
                dve.tensor_scalar(slots[w][:, :, :], slot8[:, :, 0:TOP_K], 1.0, None, ALU.subtract).then_inc(slots_ready, 1)

            def plan_experts(w):
                at = PLAN_STEPS * w
                ended = work[0:1, 0:NPAIR * E].rearrange("p (g e) -> p g e", g=NPAIR)
                dve.tensor_tensor(pairs_end[:, :], first_pair[:, :], n_pairs[:, :], ALU.add).then_inc(plan_step, 1)
                dve.wait_ge(plan_step, at + 9)
                dve.tensor_tensor(ended, pair_no[0:1, :].unsqueeze(2).to_broadcast([1, NPAIR, E]),
                                  pairs_end[0:1, :].unsqueeze(1).to_broadcast([1, NPAIR, E]), ALU.is_ge).then_inc(plan_step, 1)
                dve.wait_ge(plan_step, at + 10)
                dve.tensor_reduce(pair_expert_f[:, :], ended, AX_X, ALU.add).then_inc(plan_step, 1)
                dve.wait_ge(plan_step, at + 11)
                dve.tensor_scalar(pair_expert_f[:, :], pair_expert_f[:, :], float(E - 1), float(SHARED),
                                  ALU.min, ALU.add).then_inc(plan_step, 1)
                dve.wait_ge(plan_step, at + 12)
                dve.tensor_copy(pair_chunk[:, NPAIR * w:NPAIR * (w + 1), 0], pair_expert_f[:, :]).then_inc(experts_ready, 1)

            def plan_weights(w):
                at = PLAN_STEPS * w
                for h in range(2):
                    rows = slice(WT // 2 * h, WT // 2 * (h + 1))
                    tiles = c_all[:, WB * w + WB // 2 * h:WB * w + WB // 2 * (h + 1), :, :].rearrange("p b t e -> p (b t) e")
                    by_slot = [P, WT // 2, TOP_K, E]
                    match = work[:, 0:WT // 2 * TOP_K * E].rearrange("p (t k e) -> p t k e", t=WT // 2, k=TOP_K)
                    if h == 1:
                        dve.wait_ge(c_of_slot_ready, 2 * w + 1)
                    else:
                        dve.wait_ge(experts_ready, w + 1)
                    dve.tensor_tensor(match, slot_of[:, rows, :].unsqueeze(2).to_broadcast(by_slot),
                                      slot8[:, rows, 0:TOP_K].unsqueeze(3).to_broadcast(by_slot),
                                      ALU.is_equal).then_inc(weight_step, 1)
                    dve.wait_ge(weight_step, 4 * w + 2 * h + 1)
                    dve.tensor_tensor(match, match, tiles.unsqueeze(2).to_broadcast(by_slot), ALU.mult).then_inc(weight_step, 1)
                    dve.wait_ge(weight_step, 4 * w + 2 * h + 2)
                    dve.tensor_reduce(c_of_slot[w][:, rows, :], match, AX_X, ALU.add).then_inc(c_of_slot_ready, 1)

            def batch(b, prev, prev2, nxt, plan=None):
                if prev:
                    apply_gate(b - 1, prev2)
                if prev2:
                    routing_tail(b - 2)
                if plan == "slots":
                    plan_slots(0)
                if plan == "experts":
                    plan_experts(0)
                kv_bias(b, 0, prev)
                kv_bias(b, 1, prev)
                if prev:
                    residual(b - 1, prev2)
                kv_bias(b, 2, prev)
                kv_bias(b, 3, prev)
                dve.wait_ge(kv_biased, TT * (b + 1))
                dve.tensor_scalar(k_min[:, :, :], kv[:, :, 0:D], 0.0, None, ALU.min).then_inc(k_min_ready, 1)
                if prev:
                    normalize(x1_rows, x1_rows, b - 1, x1_ready)
                if nxt:
                    x_plus_bias(b + 1)
                    xt_lo(b + 1)

                def q_minimum(c):
                    dve.wait_ge(q_relu_ready, KC * b + c + 1)
                    if prev:
                        dve.wait_ge(q_ready, KC * b)
                    dve.tensor_scalar(q_min[:, c, :], qg_bank[c][:, :], b_q[:, c:c + 1], 0.0,
                                      ALU.add, ALU.min).then_inc(q_min_ready, 1)

                q_minimum(0)
                dve.wait_ge(k_exp_ready, b + 1)
                dve.scalar_tensor_tensor(kv[:, :, 0:D], kv[:, :, 0:D], 0.0, k_min[:, :, :],
                                         ALU.max, ALU.add).then_inc(k_ready, 1)
                q_minimum(1)
                if prev:
                    x1t_lo(b - 1)
                dve.wait_ge(kv_summed, b + 1)
                if prev:
                    dve.wait_ge(attended, KC * b)
                dve.tensor_tensor(kv_heads[:, :, :], kv_bank[0][:, 0:KC * P].rearrange("p (c n) -> p c n", c=KC),
                                  head_mask[:, :, :], ALU.mult).then_inc(kv_heads_ready, 1)
                if prev:
                    routing_head(b - 1)
                if plan == "copy":
                    plan_copy(0)

            dve.wait_ge(const_ready, 6)
            dve.wait_ge(small_loaded, 16 * 8)
            dve.tensor_copy(before[:, :], before_f).then_inc(count_consts_ready, 1)
            dve.memset(ones[:, :], 1.0).then_inc(count_consts_ready, 1)
            x_plus_bias(0)
            xt_lo(0)
            for k in range(2):
                half = slice(2 * D * k, 2 * D * (k + 1))
                dve.wait_ge(wa_hi_ready, k + 1)
                dve.tensor_tensor(wa_lo[:, :, half], wa_stage[:, :, half], wa_hi[:, :, half],
                                  ALU.subtract).then_inc(wa_lo_ready, 1)
            dve.wait_ge(gw_hi_ready, 1)
            dve.tensor_tensor(gwT_lo[:, :, :], y_bank[0][:, 0:KC * E].rearrange("p (c e) -> p c e", c=KC),
                              gwT_hi[:, :, :], ALU.subtract).then_inc(gw_lo_ready, 1)
            dve.wait_ge(wa_lo_ready, 2)
            dve.memset(wa_flat[:, :], 0.0).then_inc(zeros_ready, 1)
            batch(0, False, False, True)
            batch(1, True, False, True)
            with dve.Fori(2, 5) as b:
                batch(b, True, True, True)
            batch(5, True, True, True, plan="copy")
            batch(6, True, True, True, plan="slots")
            batch(7, True, True, False, plan="experts")
            apply_gate(NB - 1, True)
            routing_tail(NB - 2)

            def shared_hidden(g, par):
                dve.wait_ge(silu_ready, g + 1)
                dve.wait_ge(h3_ready, g + 1)
                if late(g, 1):
                    dve.wait_ge(a_lo_ready, g)
                dve.tensor_tensor(a_act[:, :], h_banks[par][1][:, :], s_act[:, :], ALU.mult).then_inc(a_ready, 1)
                dve.wait_ge(a_hi_ready, g + 1)
                dve.tensor_tensor(a_lo[par][:, :], a_act[:, :], a_hi[par][:, :], ALU.subtract).then_inc(a_lo_ready, 1)

            def add_shared(n):
                dve.wait_ge(dispatched[n], 16 * TT * TOP_K)
                dve.wait_ge(down_done, n + 1)
                if n >= WB:
                    dve.wait_ge(combined, TOP_K * (WT + 2 * (n - WB) + 1))
                for h in range(2):
                    last = dve.tensor_tensor(x_all[:, n, 2 * h:2 * h + 2, :],
                                             y_bank[h][:, :].rearrange("p (t d) -> p t d", t=2),
                                             x_all[:, n, 2 * h:2 * h + 2, :], ALU.add)
                last.then_inc(shared_added, 1)

            shared_hidden(0, 0)
            residual(NB - 1, True)
            shared_hidden(1, 1)
            normalize(x1_rows, x1_rows, NB - 1, x1_ready)
            x1t_lo(NB - 1)
            shared_hidden(2, 0)
            routing_head(NB - 1)
            add_shared(0)
            shared_hidden(3, 1)
            routing_tail(NB - 1)
            shared_hidden(4, 0)
            add_shared(1)
            plan_weights(0)
            shared_hidden(5, 1)
            plan_copy(1)
            shared_hidden(6, 0)
            plan_slots(1)
            add_shared(2)
            shared_hidden(7, 1)
            plan_experts(1)
            add_shared(3)

            def xst_lo(g, r):
                dve.wait_ge(xst_hi_ready, g + 1)
                dve.tensor_tensor(xsT_lo[r % 2][:, :, :], t_bank[r % 2][:, :].rearrange("p (c n) -> p c n", c=KC),
                                  xsT_hi[r % 2][:, :, :], ALU.subtract).then_inc(xst_lo_ready, 1)

            def pair(g, r, ahead=True):
                if ahead:
                    xst_lo(g + 1, r + 1)
                dve.wait_ge(pair_silu_ready, g + 1)
                if late(g, 1):
                    dve.wait_ge(at_lo_ready, g)
                dve.tensor_tensor(a_pair[:, :], h_banks[r % 2][0][:, 2 * P:], s_pair[:, :], ALU.mult).then_inc(pair_a_ready, 1)
                dve.wait_ge(at_hi_ready, g + 1)
                dve.tensor_tensor(aT_lo[r % 2][:, :], a_pair[:, :], aT_hi[r % 2][:, :], ALU.subtract).then_inc(at_lo_ready, 1)

            def combine(w, b, t):
                for j in range(TOP_K):
                    if j == 0:
                        dve.wait_ge(y_gathered[t], 16 * TOP_K * (b + 1))
                    if late(b, 1) or t > 0 or j > 0:
                        dve.wait_ge(combined, TOP_K * (TT * b + t) + j)
                    weight = c_of_slot[w][:, TT * (b - WB * w) + t, j:j + 1]
                    dve.scalar_tensor_tensor(x_all[:, b, t, :], y_got[t][:, j, :], weight, x_all[:, b, t, :],
                                             ALU.mult, ALU.add).then_inc(combined, 1)

            def final_stats(b):
                dve.wait_ge(combined, TOP_K * TT * (b + 1))
                dve.memset(wait_pad[:, :], 0.0)
                norm_stats(lambda t: x_all[:, b, t, :], NB + b)

            def final_norm(b):
                if late(b, 1):
                    dve.wait_ge(out_stored, 16 * b)
                normalize(lambda t: x_all[:, b, t, :], lambda t: o_sb[:, t, :], NB + b, out_ready)

            def group(q, adds=(), norm=None, stats=None, last=False):
                for r in range(RING):
                    pair(RING * q + r, r, not (last and r == RING - 1))
                    if adds and r % 2 == 1:
                        combine(0, *adds[r // 2])
                if norm is not None:
                    final_norm(norm)
                if stats is not None:
                    final_stats(stats)

            q1 = GROUPS_OF_PAIRS
            xst_lo(0, 0)
            group(0)
            with dve.Fori(1, q1 + 1) as q:
                group(q)
            dve.wait_ge(c_of_slot_ready, 2)
            dve.wait_ge(shared_added, WB)
            group(q1 + 1, [(0, 0), (0, 1)])
            group(q1 + 2, [(0, 2), (0, 3)], stats=0)
            with dve.Fori(1, WB) as b:
                group(q1 + 1 + 2 * b, [(b, 0), (b, 1)], norm=b - 1)
                group(q1 + 2 + 2 * b, [(b, 2), (b, 3)], stats=b)
            group(q1 + 1 + 2 * WB, norm=WB - 1)
            with dve.Fori(q1 + 2 + 2 * WB, WAVES * q1 - 1) as q:
                group(q)
            group(WAVES * q1 - 1, last=True)
            plan_weights(1)

            dve.wait_ge(c_of_slot_ready, 4)
            tiles = [(b, t) for b in range(WB, NB) for t in range(TT)]
            for n in range(WB, NB):
                shared_hidden(SHARED * n, 0)
                if n > WB:
                    add_shared(n - 1)
                    dve.wait_ge(shared_added, n)
                combine(1, *tiles[2 * (n - WB)])
                shared_hidden(SHARED * n + 1, 1)
                combine(1, *tiles[2 * (n - WB) + 1])
                if n == WB + 1:
                    final_stats(WB)
                if n == NB - 1:
                    final_norm(WB)
                    final_stats(WB + 1)
            add_shared(NB - 1)
            dve.wait_ge(shared_added, NB)
            for b in range(WB + 2, NB):
                for t in range(TT):
                    combine(1, b, t)
                    if t == 1:
                        final_norm(b - 1)
                final_stats(b)
            final_norm(NB - 1)

        @block.tensor
        def _(pe):
            def product(dst, sta_hi, sta_lo, mov_hi, mov_lo, start, stop):
                pe.matmul(dst, sta_hi, mov_hi, start=start, stop=False)
                pe.matmul(dst, sta_hi, mov_lo, start=False, stop=False)
                return pe.matmul(dst, sta_lo, mov_hi, start=False, stop=stop)

            def transpose_x(src, done):
                for c in range(KC):
                    for t in range(TT):
                        last = pe.transpose(t_bank[c][:, t * P:(t + 1) * P], src[:, t, c * P:(c + 1) * P],
                                            ident[:, :])
                    last.then_inc(done, 1)

            def project_kv(b, t):
                if not (isinstance(b, int) and b == 0) or t >= 2:
                    pe.wait_ge(kv_biased, TT * b + t - 1)
                if not (isinstance(b, int) and b == 0) and t == 0:
                    pe.wait_ge(kv_heads_ready, b)
                tok = slice(t * P, (t + 1) * P)
                for c in range(KC):
                    last = product(kv_bank[t % 2][:, :], xT_hi[:, c, b, tok], xT_lo[:, c, b, tok],
                                   wa_hi[:, c, 0:2 * D], wa_lo[:, c, 0:2 * D], c == 0, c == KC - 1)
                last.then_inc(kv_projected, 1)

            def project_features(b, m, col, done):
                cols = slice(col + m * P, col + (m + 1) * P)
                for c in range(KC):
                    last = product(qg_bank[m][:, :], wa_hi[:, c, cols], wa_lo[:, c, cols],
                                   xT_hi[:, c, b, :], xT_lo[:, c, b, :], c == 0, c == KC - 1)
                last.then_inc(done, 1)

            def project_out(b):
                for h in range(2):
                    pe.wait_ge(gated_ready, KC * (b + 1))
                    for t in range(2 * h, 2 * h + 2):
                        for c in range(KC):
                            last = pe.matmul(y_bank[h][:, (t % 2) * D:(t % 2 + 1) * D],
                                             gated[:, c, t * P:(t + 1) * P], wo_sb[:, c, :],
                                             start=c == 0, stop=c == KC - 1)
                    last.then_inc(wo_projected, 1)

            def sum_kv(b):
                pe.wait_ge(k_ready, b + 1)
                for c in range(KC):
                    for t in range(TT):
                        last = pe.matmul(kv_bank[0][:, c * P:(c + 1) * P], kv[:, t, c * P:(c + 1) * P],
                                         kv[:, t, D + c * P:D + (c + 1) * P], start=t == 0, stop=t == TT - 1)
                last.then_inc(kv_summed, 1)

            def attend(b):
                pe.wait_ge(kv_heads_ready, b + 1)
                pe.wait_ge(q_ready, KC * (b + 1))
                for c in range(KC):
                    pe.matmul(y_bank[c][:, :], kv_heads[:, c, :], q_fm[:, c, :], start=True,
                              stop=True).then_inc(attended, 1)

            def route(b):
                pe.wait_ge(x1t_lo_ready, KC * (b + 1))
                for t in range(TT):
                    dst = t_bank[1][:, t * E:(t + 1) * E]
                    for c in range(KC):
                        hi, lo = xT_hi[:, c, b, t * P:(t + 1) * P], xT_lo[:, c, b, t * P:(t + 1) * P]
                        pe.matmul(dst, hi, gwT_hi[:, c, :], start=c == 0, stop=False)
                        pe.matmul(dst, hi, gwT_lo[:, c, :], start=False, stop=False)
                        pe.matmul(dst, lo, gwT_hi[:, c, :], start=False, stop=False)
                        last = pe.matmul(dst, lo, gwT_lo[:, c, :], start=False, stop=c == KC - 1)
                last.then_inc(logits_ready, 1)

            def count_tokens(w):
                pe.wait_ge(count_consts_ready, 2)
                pe.wait_ge(c_ready, WB * (w + 1))
                counts = t_bank[0][:, 0:(WT + 1) * E].rearrange("p (t e) -> p t e", e=E)
                chosen = sel_all[:, WB * w:WB * (w + 1), :, :].rearrange("p b t e -> p (b t) e")
                for t in range(WT + 1):
                    for u in range(min(t, WT)):
                        last = pe.matmul(counts[:, t, :], ones[:, :], chosen[:, u, :], start=u == 0,
                                         stop=u == WT - 1 and t == WT)
                    if t < WT:
                        pe.matmul(counts[:, t, :], before[:, :], chosen[:, t, :], start=t == 0, stop=True)
                last.then_inc(counted, 1)

            def batch(b, prev, prev2, nxt, plan=False):
                pe.wait_ge(xt_lo_ready, KC * (b + 1))
                project_kv(b, 0)
                project_kv(b, 1)
                if prev:
                    project_out(b - 1)
                project_kv(b, 2)
                project_kv(b, 3)
                if nxt:
                    pe.wait_ge(x_loaded, 16 * (b + 2))
                if prev2:
                    pe.wait_ge(x1t_lo_ready, KC * (b - 1))
                    if isinstance(b, int) and b == 6:
                        pe.wait_ge(plan_copied, 1)
                    pe.wait_ge(gating_step, GATING_STEPS * (b - 2) + 2)
                if nxt:
                    transpose_x(x_in, x_transposed)
                if prev:
                    pe.wait_ge(gate_ready, KC * b)
                project_features(b, 0, 2 * D, q_projected)
                project_features(b, 1, 2 * D, q_projected)
                if nxt:
                    pe.wait_ge(xt_lo_ready, KC * (b + 2))
                if prev:
                    pe.wait_ge(x1_ready, b)
                    transpose_x(x1_sb, x1_transposed)
                pe.wait_ge(q_min_ready, KC * b + 1)
                pe.wait_ge(q_relu_ready, KC * b + 1)
                project_features(b, 0, 3 * D, g_projected)
                sum_kv(b)
                pe.wait_ge(q_min_ready, KC * b + 2)
                pe.wait_ge(q_relu_ready, KC * b + 2)
                project_features(b, 1, 3 * D, g_projected)
                if prev:
                    route(b - 1)
                    pe.wait_ge(residual_ready, 2 * b)
                attend(b)
                if plan:
                    count_tokens(0)

            pe.wait_ge(const_ready, 6)
            pe.wait_ge(x_loaded, 16)
            transpose_x(x_in, x_transposed)
            pe.wait_ge(small_loaded, 16 * 8)
            for c in range(KC):
                last = pe.transpose(y_bank[0][:, c * E:(c + 1) * E], gw_sb[:, c * P:(c + 1) * P], ident[0:E, 0:E])
            last.then_inc(gw_transposed, 1)
            pe.wait_ge(wa_lo_ready, 2)
            pe.wait_ge(gw_lo_ready, 1)
            batch(0, False, False, True)
            batch(1, True, False, True)
            with pe.Fori(2, 5) as b:
                batch(b, True, True, True)
            batch(5, True, True, True, plan=True)
            batch(6, True, True, True)
            batch(NB - 1, True, True, False)

            def up(g, n, par):
                if late(g, 2):
                    pe.wait_ge(a_ready, g - 1)
                for k, done in enumerate((h1_ready, h3_ready)):
                    for c in range(KC):
                        cols = slice((c * 2 + k) * INTER, (c * 2 + k + 1) * INTER)
                        last = product(h_banks[par][k][:, :], we_hi[:, par, cols], we_lo[:, par, cols],
                                       xT_hi[:, c, n, :], xT_lo[:, c, n, :], c == 0, c == KC - 1)
                    last.then_inc(done, 1)

            def down(n):
                pe.wait_ge(a_lo_ready, SHARED * (n + 1))
                if late(n, 1):
                    pe.wait_ge(shared_added, n)
                for t in range(TT):
                    tok = slice(t * P, (t + 1) * P)
                    for j in range(SHARED):
                        last = product(y_bank[t // 2][:, (t % 2) * D:(t % 2 + 1) * D], a_hi[j][:, tok], a_lo[j][:, tok],
                                       we_hi[:, j, W13:], we_lo[:, j, W13:], j == 0, j == SHARED - 1)
                last.then_inc(down_done, 1)

            pe.wait_ge(we_lo_ready, PAIRS)
            pe.wait_ge(kv_biased, TT * NB)
            pe.wait_ge(kv_heads_ready, NB)
            up(0, 0, 0)
            project_out(NB - 1)
            pe.wait_ge(gate_ready, KC * NB)
            up(1, 0, 1)
            up(2, 1, 0)
            pe.wait_ge(x1_ready, NB)
            pe.wait_ge(x1t_lo_ready, KC * (NB - 1))
            pe.wait_ge(gating_step, GATING_STEPS * (NB - 2) + 2)
            transpose_x(x1_sb, x1_transposed)
            pe.wait_ge(residual_ready, 2 * NB)
            down(0)
            route(NB - 1)
            up(3, 1, 1)
            up(4, 2, 0)
            down(1)
            up(5, 2, 1)
            count_tokens(1)
            up(6, 3, 0)
            down(2)
            up(7, 3, 1)
            down(3)

            def transpose_xs(g, r, use):
                pe.wait_ge(xs_loaded[r], 16 * use)
                if late(g, 2):
                    pe.wait_ge(xst_lo_ready, g - 1)
                for c in range(KC):
                    for i in range(2):
                        last = pe.transpose(t_bank[r % 2][:, c * 2 * P + i * P:c * 2 * P + (i + 1) * P],
                                            xs[r][:, i, c * P:(c + 1) * P], ident[:, :])
                last.then_inc(xs_transposed, 1)

            def chunk_of(g):
                return pe.value_load(pair_chunk[0:1, g, :], min_val=SHARED, max_val=NCH - 1)

            def up_pair(g, r, chunk):
                pe.wait_ge(xst_lo_ready, g + 1)
                if late(g, 2):
                    pe.wait_ge(pair_a_ready, g - 1)
                for k in range(2):
                    for c in range(KC):
                        cols = slice((c * 2 + k) * INTER, (c * 2 + k + 1) * INTER)
                        last = product(h_banks[r % 2][0][:, k * PAIR:(k + 1) * PAIR],
                                       we_hi[:, chunk, cols], we_lo[:, chunk, cols],
                                       xsT_hi[r % 2][:, c, :], xsT_lo[r % 2][:, c, :], c == 0, c == KC - 1)
                last.then_inc(h_ready, 1)

            def down_pair(g, r, chunk):
                pe.wait_ge(at_lo_ready, g + 1)
                if late(g, 2):
                    pe.wait_ge(ys_copied, g - 1)
                w2_hi, w2_lo = we_hi[:, chunk, W13:], we_lo[:, chunk, W13:]
                dst, tok = y_bank[r % 2][:, 0:D], slice(0, P)
                pe.matmul(dst, aT_hi[r % 2][:, tok], w2_hi, start=True, stop=False)
                pe.matmul(dst, aT_lo[r % 2][:, tok], w2_hi, start=False, stop=False)
                pe.matmul(dst, aT_hi[r % 2][:, tok], w2_lo, start=False, stop=True)
                dst, tok = y_bank[r % 2][:, D:], slice(P, PAIR)
                pe.matmul(dst, aT_hi[r % 2][:, tok], w2_lo, start=True, stop=False)
                pe.matmul(dst, aT_hi[r % 2][:, tok], w2_hi, start=False, stop=False)
                pe.matmul(dst, aT_lo[r % 2][:, tok], w2_hi, start=False, stop=True).then_inc(ys_ready, 1)

            def group(q, last=False):
                for r in range(RING):
                    g = RING * q + r
                    if r > 0:
                        before_this = chunk
                    elif late(q, 1):
                        before_this = chunk_of(g - 1)
                    chunk = chunk_of(g)
                    if not (last and r == RING - 1):
                        transpose_xs(g + 1, (r + 1) % RING, q + 1 + (r + 1) // RING)
                    up_pair(g, r, chunk)
                    if r > 0 or late(q, 1):
                        down_pair(g - 1, (r - 1) % RING, before_this)
                return chunk

            all_groups = WAVES * GROUPS_OF_PAIRS
            pe.wait_ge(experts_ready, 1)
            pe.wait_ge(plan_copied, WAVES)
            pe.wait_ge(gating_step, GATING_STEPS * (NB - 1) + 2)
            transpose_xs(0, 0, 1)
            pe.wait_ge(a_ready, SHARED * WB)
            pe.wait_ge(shared_added, WB)
            group(0)
            with pe.Fori(1, GROUPS_OF_PAIRS) as q:
                group(q)
            pe.wait_ge(experts_ready, 2)
            with pe.Fori(GROUPS_OF_PAIRS, all_groups - 1) as q:
                group(q)
            chunk = group(all_groups - 1, last=True)
            pe.wait_ge(pair_a_ready, RING * all_groups - 1)
            up(SHARED * WB, WB, 0)
            down_pair(RING * all_groups - 1, RING - 1, chunk)
            pe.wait_ge(pair_a_ready, RING * all_groups)
            up(SHARED * WB + 1, WB, 1)
            pe.wait_ge(ys_copied, RING * all_groups)
            with pe.Fori(WB + 1, NB) as n:
                up(SHARED * n, n, 0)
                down(n - 1)
                up(SHARED * n + 1, n, 1)
            down(NB - 1)


_INS = ["L0_attn_x", "L0_attn_Wq", "L0_attn_bq", "L0_attn_Wk", "L0_attn_bk", "L0_attn_Wv", "L0_attn_bv",
        "L0_attn_Wg", "L0_attn_bg", "L0_attn_Wo", "L0_attn_bo", "L0_ffn_gate_w", "L0_ffn_w1", "L0_ffn_w2",
        "L0_ffn_w3", "L0_ffn_ws1", "L0_ffn_ws2", "L0_ffn_ws3"]


def _plan_constants(np, token_tiles, experts):
    pairs = token_tiles * TOP_K // 2 + experts
    before = np.triu(np.ones((P, P)), 1)
    earlier_e = np.tril(np.ones((experts, experts)), -1).reshape(1, -1)
    starts = 2 * P * np.arange(token_tiles // 2).reshape(1, -1)
    pair_no = np.arange(pairs).reshape(1, -1)
    rows = [np.broadcast_to(a, (P, a.shape[1])) for a in (before, earlier_e, starts, pair_no)]
    return np.concatenate(rows, axis=1).astype(np.float32)


def kernel(**inputs):
    import numpy as _np
    import concourse.bacc as _bacc
    from concourse.bass_utils import run_bass_kernel_spmd as _run

    nc = _bacc.Bacc("TRN2", target_bir_lowering=False, num_devices=1)
    arrays, args = {}, []
    tokens_sent = inputs["L0_attn_x"].shape[0] * inputs["L0_attn_x"].shape[1] // 2
    experts = inputs["L0_ffn_gate_w"].shape[0]
    sources = dict(inputs, plan_consts=_plan_constants(_np, tokens_sent // P, experts))
    for name in _INS + ["plan_consts"]:
        a = _np.ascontiguousarray(sources[name])
        arrays[f"in_{name}"] = a
        args.append(nc.dram_tensor(f"in_{name}", a.shape, mybir.dt.from_np(a.dtype), kind="ExternalInput").ap())
    shape = arrays["in_L0_attn_x"].shape
    args.append(nc.dram_tensor("out_0", shape, F32, kind="ExternalOutput").ap())
    attention_and_experts(nc, *args)
    r = _run(nc, [arrays], core_ids=[0])
    return r.results[0]["out_0"]
```

```python
from contextlib import ExitStack

import concourse.bass as bass
from concourse import mybir

F32 = mybir.dt.float32
HI = mybir.dt.float16
LO = mybir.dt.bfloat16
U32 = mybir.dt.uint32
I32 = mybir.dt.int32
ALU = mybir.AluOpType
ACT = mybir.ActivationFunctionType
AX_X = mybir.AxisListType.X

P = 128
PLAN_PARTS = 22
PLAN_STEPS = 12
SLOTS_READY_PART, WEIGHTS_PART = 12, 16
LN_EPS = 1e-5
HDIM = 16
GROUPS = 4
TOP_GROUPS = 2
TOP_K = 4
TAKEN = -1.0
FILLER = -2.0

GATING_STEPS = 15


def attention_and_experts(nc: bass.Bass, x, Wq, bq, Wk, bk, Wv, bv, Wg, bg, Wo, bo,
                          gate_w, w1, w2, w3, ws1, ws2, ws3, plan_consts, out):
    NB, S, D = x.shape
    KC = D // P
    TT = S // P
    E, _, INTER = w1.shape
    SHARED = ws1.shape[1] // INTER
    NCH = SHARED + E
    PAIRS = NCH // 2
    WAVES = 2
    WB = NB // WAVES
    WT = WB * TT
    NPAIR = WT * TOP_K // 2 + E
    PAIR = 2 * P
    SLOTS = NPAIR * PAIR
    MOST = WT // 2
    RING = 4
    GROUPS_OF_PAIRS = NPAIR // RING
    EARLY = WB - 1
    PLAN_GROUPS = 7
    FILL_ROWS = 512
    FILLS = SLOTS // FILL_ROWS
    FILLS_AT = 2
    FILLS_LATE = 8
    assert (P, KC, TT, E, INTER, SHARED) == (128, 2, 4, 16, 128, 2) and NPAIR == RING * GROUPS_OF_PAIRS
    assert NB == 8 and WAVES == 2 and PAIRS == 9 and S == 512 and GROUPS_OF_PAIRS == 2 * WB + 4
    assert WAVES * FILLS <= 12 * FILLS_AT + 3 * FILLS_LATE and SLOTS == FILLS * FILL_ROWS
    W13 = 2 * KC * INTER
    WCOLS = W13 + D
    EG = E // GROUPS

    xs_dram = [nc.dram_tensor(f"expert_in{w}", (SLOTS, D), F32, kind="Internal").ap() for w in range(WAVES)]
    ys_dram = [nc.dram_tensor(f"expert_out{w}", (SLOTS, D), F32, kind="Internal").ap() for w in range(WAVES)]

    with ExitStack() as ctx:
        def sb(name, shape, dt=F32):
            return ctx.enter_context(nc.sbuf_tensor(name, shape, dt))

        def bank(name):
            return ctx.enter_context(nc.psum_tensor(name, [P, 512], F32))

        def sem(name):
            return ctx.enter_context(nc.semaphore(name))

        x_all = sb("x_all", [P, NB, TT, D])
        x_in = sb("x_in", [P, TT, D])
        x1_sb = sb("x1_sb", [P, TT, D])
        xT_hi = sb("xT_hi", [P, KC, NB, S], HI)
        xT_lo = sb("xT_lo", [P, KC, NB, S], LO)
        wa_hi = sb("wa_hi", [P, KC, 4 * D], HI)
        wa_lo = sb("wa_lo", [P, KC, 4 * D], LO)
        wo_sb = sb("wo_sb", [P, KC, D])
        we_hi = sb("we_hi", [P, NCH, WCOLS], HI)
        we_lo = sb("we_lo", [P, NCH, WCOLS], LO)
        stage = sb("stage", [P, 2, WCOLS])
        wa_stage = sb("wa_stage", [P, KC, 4 * D])
        wa_flat = wa_stage[:, :, :].rearrange("p c n -> p (c n)")
        zeros = wa_flat[:, 0:FILL_ROWS * D // P]
        ident = sb("ident", [P, P])
        head_mask = sb("head_mask", [P, KC, P])
        earlier = sb("earlier", [P, TT, GROUPS, GROUPS])
        minus_half = sb("minus_half", [P, TT])
        eps = sb("eps", [P, TT])
        b_kv = sb("b_kv", [P, 2 * D])
        b_o = sb("b_o", [P, D])
        b_q = sb("b_q", [P, KC])
        b_g = sb("b_g", [P, KC])
        gw_sb = sb("gw_sb", [E, D])
        gwT_hi = sb("gwT_hi", [P, KC, E], HI)
        gwT_lo = sb("gwT_lo", [P, KC, E], LO)
        kv = sb("kv", [P, TT, 2 * D])
        k_min = sb("k_min", [P, TT, D])
        q_exp = sb("q_exp", [P, KC, S])
        q_fm = sb("q_fm", [P, KC, S])
        gate = sb("gate", [P, KC, S])
        gated = sb("gated", [P, KC, S])
        kv_heads = sb("kv_heads", [P, KC, P])
        wait_pad = sb("wait_pad", [P, 1])
        bn = sb("bn", [P, TT, 6])
        mv = sb("mv", [P, TT, 2])
        var_eps = sb("var_eps", [P, TT])
        rstd = sb("rstd", [P, TT])
        r_max = sb("r_max", [P, TT])
        r_sub = sb("r_sub", [P, TT, E])
        r_exp = sb("r_exp", [P, TT, E])
        r_sum = sb("r_sum", [P, TT])
        r_inv = sb("r_inv", [P, TT])
        score = sb("score", [P, TT, E])
        g_max = sb("g_max", [P, TT, GROUPS])
        g_gt = sb("g_gt", [P, TT, GROUPS, GROUPS])
        g_eq = sb("g_eq", [P, TT, GROUPS, GROUPS])
        g_rank = sb("g_rank", [P, TT, GROUPS])
        g_sel = sb("g_sel", [P, TT, GROUPS])
        masked = sb("masked", [P, TT, E + 8 - TOP_K])
        top8 = sb("top8", [P, TT, 8])
        marked = sb("marked", [P, TT, E + 8 - TOP_K])
        sel_all = sb("sel_all", [P, NB, TT, E], HI)
        c_all = sb("c_all", [P, NB, TT, E])
        plan_sb = sb("plan_sb", [P, P + E * E + MOST + NPAIR])
        before_f = plan_sb[:, 0:P]
        earlier_e = plan_sb[:, P:P + E * E].rearrange("p (e f) -> p e f", e=E)
        starts = plan_sb[:, P + E * E:P + E * E + MOST]
        pair_no = plan_sb[:, P + E * E + MOST:]
        before = sb("before", [P, P], HI)
        ones = sb("ones", [P, P], HI)
        prefix = sb("prefix", [P, (WT + 1) * E])
        work = stage[:, :, :].rearrange("p s n -> p (s n)")
        n_pairs = sb("n_pairs", [P, E])
        first_pair = sb("first_pair", [P, E])
        pairs_end = sb("pairs_end", [P, E])
        first_slot = sb("first_slot", [P, E])
        slot_of = [sb(f"slot_of{w}", [P, WT, E]) for w in range(WAVES)]
        slot8 = [sb(f"slot8_{w}", [P, WT, 8]) for w in range(WAVES)]
        slots = [sb(f"slots{w}", [P, WT, TOP_K], U32) for w in range(WAVES)]
        c_of_slot = [sb(f"c_of_slot{w}", [P, WT, TOP_K]) for w in range(WAVES)]
        pair_expert_f = sb("pair_expert_f", [1, NPAIR])
        pair_chunk = sb("pair_chunk", [1, WAVES * NPAIR, 1], I32)
        a_hi = [sb(f"a_hi{i}", [P, S], HI) for i in range(2)]
        a_lo = [sb(f"a_lo{i}", [P, S], LO) for i in range(2)]
        xsT_hi = [sb(f"xsT_hi{i}", [P, KC, 2 * P], HI) for i in range(2)]
        xsT_lo = [sb(f"xsT_lo{i}", [P, KC, 2 * P], LO) for i in range(2)]
        xs = [kv[:, r, :].rearrange("p (t d) -> p t d", t=2) for r in range(RING)]
        flat = "p c n -> p (c n)"
        ys = [buf[:, :, :].rearrange(flat)[:, i * 2 * D:(i + 1) * 2 * D].rearrange("p (t d) -> p t d", t=2)
              for buf in (k_min, q_exp) for i in range(2)]
        y_got = [buf[:, :, :].rearrange(flat).rearrange("p (k d) -> p k d", k=TOP_K) for buf in (q_fm, gate)]
        y_got += [wa_flat[:, i * TOP_K * D:(i + 1) * TOP_K * D].rearrange("p (k d) -> p k d", k=TOP_K)
                  for i in range(2)]
        o_sb = gated[:, :, :].rearrange(flat).rearrange("p (t d) -> p t d", t=TT)
        a_hi += [wa_hi[:, 0, i * S:(i + 1) * S] for i in range(2)]
        a_lo += [wa_lo[:, 0, i * S:(i + 1) * S] for i in range(2)]
        aT_hi = [wa_hi[:, 1, i * PAIR:(i + 1) * PAIR] for i in range(2)]
        aT_lo = [wa_lo[:, 1, i * PAIR:(i + 1) * PAIR] for i in range(2)]
        s_act = x_in[:, :, :].rearrange(flat)[:, 0:S]
        a_act = x_in[:, :, :].rearrange(flat)[:, S:2 * S]
        s_pair, a_pair = x1_sb[:, 0, :], x1_sb[:, 1, :]

        h_banks = [[bank("h1_even"), bank("h3_even")], [bank("h1_odd"), bank("h3_odd")]]
        kv_bank = h_banks[0]
        qg_bank = h_banks[1]
        y_bank = [bank("y0"), bank("y1")]
        t_bank = [bank("t0"), bank("t1")]
        count_bank = [t_bank[0], h_banks[0][1]]

        x_loaded, wa_loaded, small_loaded = sem("x_loaded"), sem("wa_loaded"), sem("small_loaded")
        stage_loaded, out_stored = sem("stage_loaded"), sem("out_stored")
        zeros_ready = sem("zeros_ready")
        zero_filled = [sem(f"zero_filled{w}") for w in range(WAVES)]
        dispatched = [sem(f"dispatched{b}") for b in range(NB)]
        xs_loaded = [sem(f"xs_loaded{r}") for r in range(RING)]
        ys_stored = [sem(f"ys_stored{r}") for r in range(RING)]
        y_gathered = [sem(f"y_gathered{i}") for i in range(RING)]
        const_step, const_ready = sem("const_step"), sem("const_ready")
        wa_hi_ready, wa_lo_ready = sem("wa_hi_ready"), sem("wa_lo_ready")
        gw_transposed, gw_hi_ready, gw_lo_ready = sem("gw_transposed"), sem("gw_hi_ready"), sem("gw_lo_ready")
        we_hi_ready, we_lo_ready = sem("we_hi_ready"), sem("we_lo_ready")
        x_transposed, xt_hi_ready, xt_lo_ready = sem("x_transposed"), sem("xt_hi_ready"), sem("xt_lo_ready")
        kv_projected, kv_biased = sem("kv_projected"), sem("kv_biased")
        k_min_ready, k_exp_ready, k_ready = sem("k_min_ready"), sem("k_exp_ready"), sem("k_ready")
        q_projected = sem("q_projected")
        q_exp_ready, q_ready = sem("q_exp_ready"), sem("q_ready")
        g_projected, gate_ready = sem("g_projected"), sem("gate_ready")
        kv_summed, kv_heads_ready = sem("kv_summed"), sem("kv_heads_ready")
        attended, gated_ready = sem("attended"), sem("gated_ready")
        wo_projected, x_biased, residual_ready = sem("wo_projected"), sem("x_biased"), sem("residual_ready")
        bn_ready, mv_ready, var_eps_ready, rstd_ready = sem("bn_ready"), sem("mv_ready"), sem("var_eps_ready"), sem("rstd_ready")
        x1_ready, x1_transposed, x1_kept = sem("x1_ready"), sem("x1_transposed"), sem("x1_kept")
        x1t_hi_ready, x1t_lo_ready = sem("x1t_hi_ready"), sem("x1t_lo_ready")
        logits_ready, gating_step, r_exp_ready = sem("logits_ready"), sem("gating_step"), sem("r_exp_ready")
        c_ready, counted, plan_copied, plan_step = sem("c_ready"), sem("counted"), sem("plan_copied"), sem("plan_step")
        count_consts_ready, slots_ready = sem("count_consts_ready"), sem("slots_ready")
        experts_ready, c_of_slot_ready, weight_step = sem("experts_ready"), sem("c_of_slot_ready"), sem("weight_step")
        xs_transposed, xst_hi_ready, xst_lo_ready = sem("xs_transposed"), sem("xst_hi_ready"), sem("xst_lo_ready")
        h_ready, pair_silu_ready, pair_a_ready = sem("h_ready"), sem("pair_silu_ready"), sem("pair_a_ready")
        at_hi_ready, at_lo_ready = sem("at_hi_ready"), sem("at_lo_ready")
        ys_ready, ys_copied, combined = sem("ys_ready"), sem("ys_copied"), sem("combined")
        h1_ready, h3_ready, silu_ready = sem("h1_ready"), sem("h3_ready"), sem("silu_ready")
        a_ready, a_hi_ready, a_lo_ready = sem("a_ready"), sem("a_hi_ready"), sem("a_lo_ready")
        down_done, shared_added = sem("down_done"), sem("shared_added")
        out_ready = sem("out_ready")

        def stage_sources(m):
            if isinstance(m, int) and m == 0:
                return [(ws1[:, s * INTER:(s + 1) * INTER], ws3[:, s * INTER:(s + 1) * INTER],
                         ws2[s * INTER:(s + 1) * INTER, :]) for s in range(SHARED)]
            return [(w1[2 * m - 2 + s], w3[2 * m - 2 + s], w2[2 * m - 2 + s]) for s in range(2)]

        def late(i, n):
            return not isinstance(i, int) or i >= n

        block = ctx.enter_context(nc.Block())

        @block.sync
        def _(sp):
            def load_x(b):
                sp.dma_start(x_in[:, :, :], x[b].rearrange("(t p) d -> p t d", p=P)).then_inc(x_loaded, 16)

            def load_stage(m):
                for s, (a1, a3, a2) in enumerate(stage_sources(m)):
                    for k, src in enumerate((a1, a3)):
                        dst = stage[:, s, 0:W13].rearrange("p (c k i) -> p c k i", c=KC, k=2)[:, :, k, :]
                        sp.dma_start(dst,
                                     src.rearrange("(c p) i -> p c i", p=P)).then_inc(stage_loaded, 16)
                    sp.dma_start(stage[:, s, W13:], a2).then_inc(stage_loaded, 16)

            load_x(0)
            for k, w in enumerate((Wk, Wv, Wq, Wg)):
                sp.dma_start(wa_stage[:, :, k * D:(k + 1) * D],
                             w.rearrange("(c p) n -> p c n", p=P)).then_inc(wa_loaded, 16)
            sp.dma_start(b_kv[:, 0:D], bk.partition_broadcast(P)).then_inc(small_loaded, 16)
            sp.dma_start(b_kv[:, D:], bv.partition_broadcast(P)).then_inc(small_loaded, 16)
            sp.dma_start(b_o[:, :], bo.partition_broadcast(P)).then_inc(small_loaded, 16)
            sp.dma_start(wo_sb[:, :, :], Wo.rearrange("(c p) n -> p c n", p=P)).then_inc(small_loaded, 16)
            sp.dma_start(gw_sb[:, :], gate_w).then_inc(small_loaded, 16)
            sp.dma_start(plan_sb[:, :], plan_consts).then_inc(small_loaded, 16)
            load_stage(0)

            xs_fill = [x_.rearrange("(n p r) d -> n p (r d)", p=P, r=FILL_ROWS // P) for x_ in xs_dram]
            xs_pairs = [x_.rearrange("(g t p) d -> g p t d", t=2, p=P) for x_ in xs_dram]
            ys_pairs = [y_.rearrange("(g t p) d -> g p t d", t=2, p=P) for y_ in ys_dram]

            def fill(i):
                w = i // FILLS
                sp.dma_start(xs_fill[w][i % FILLS], zeros).then_inc(zero_filled[w], 16)

            def next_x(b):
                sp.wait_ge(x_biased, b)
                load_x(b)

            def next_stage(m):
                sp.wait_ge(we_lo_ready, m)
                load_stage(m)

            next_x(1)
            next_stage(1)
            sp.wait_ge(zeros_ready, 1)
            next_x(2)
            for i in range(FILLS_AT):
                fill(i)
            next_x(3)
            next_stage(2)
            for i in range(2 * FILLS_AT):
                fill(FILLS_AT + i)
            for b in range(2, 5):
                at = 3 * FILLS_AT * (b - 1)
                next_stage(2 * b - 1)
                for i in range(FILLS_AT):
                    fill(at + i)
                next_x(b + 2)
                for i in range(FILLS_AT):
                    fill(at + FILLS_AT + i)
                next_stage(2 * b)
                for i in range(FILLS_AT):
                    fill(at + 2 * FILLS_AT + i)
            next_x(NB - 1)
            for b in range(5, NB):
                sp.wait_ge(x1_kept, b)
                at = FILLS_AT * 12 + FILLS_LATE * (b - 5)
                for i in range(at, min(at + FILLS_LATE, WAVES * FILLS)):
                    fill(i)

            def load_xs(w, p, r, first=False):
                if not first:
                    sp.wait_ge(xs_transposed, NPAIR * w + p - RING + 1)
                sp.dma_start(xs[r][:, :, :], xs_pairs[w][p]).then_inc(xs_loaded[r], 16)

            def store_ys(w, p, r):
                sp.wait_ge(ys_copied, NPAIR * w + p + 1)
                sp.dma_start(ys_pairs[w][p], ys[r][:, :, :]).then_inc(ys_stored[r], 16)

            def store_out(b):
                sp.wait_ge(out_ready, b + 1)
                sp.dma_start(out[b].rearrange("(t p) d -> p t d", p=P), o_sb[:, :, :]).then_inc(out_stored, 16)

            def group(w, q, first=False):
                for r in range(RING):
                    load_xs(w, RING * (q + 1) + r, r)
                    if r > 0:
                        store_ys(w, RING * q + r - 1, r - 1)
                    elif not first:
                        store_ys(w, RING * q - 1, RING - 1)

            last = GROUPS_OF_PAIRS - 1
            for b in range(WB):
                sp.wait_ge(dispatched[b], 16 * TT * TOP_K)
            sp.wait_ge(kv_summed, NB)
            for r in range(RING):
                load_xs(0, r, r, first=True)
            group(0, 0, first=True)
            with sp.Fori(0, (last - 1) // 2) as q2:
                group(0, 2 * q2 + 1)
                group(0, 2 * q2 + 2)
            for b in range(WB, NB):
                sp.wait_ge(dispatched[b], 16 * TT * TOP_K)
            for r in range(RING):
                load_xs(1, r, r)
                store_ys(0, RING * last + r - 1, (r - 1) % RING)
            load_xs(1, RING, 0)
            store_ys(0, RING * last + RING - 1, RING - 1)
            for r in range(1, RING):
                load_xs(1, RING + r, r)
                store_ys(1, r - 1, r - 1)
            with sp.Fori(1, 3) as q2:
                group(1, 2 * q2 - 1)
                group(1, 2 * q2)
            with sp.Fori(1, WB) as b:
                store_out(b - 1)
                group(1, 2 * b + 3)
                group(1, 2 * b + 4)
            for r in range(-1, RING):
                store_ys(1, RING * last + r, r % RING)
            with sp.Fori(WB - 1, NB) as b:
                store_out(b)
            sp.wait_ge(out_stored, 16 * NB)

        @block.gpsimd
        def _(pool):
            pool.memset(ident[:, :], 0.0).then_inc(const_step, 1)
            pool.memset(head_mask[:, :, :], 1.0).then_inc(const_step, 1)
            pool.memset(earlier[:, :, :, :], 1.0).then_inc(const_step, 1)
            pool.memset(minus_half[:, :], -0.5).then_inc(const_ready, 1)
            pool.memset(eps[:, :], LN_EPS).then_inc(const_ready, 1)
            pool.memset(masked[:, :, E:], FILLER).then_inc(const_ready, 1)
            pool.wait_ge(const_step, 3)
            pool.affine_select(out=ident[:, :], in_=ident[:, :], compare_op=ALU.not_equal, fill=1.0,
                               base=0, pattern=[[-1, P]], channel_multiplier=1).then_inc(const_ready, 1)
            pool.affine_select(out=earlier[:, :, :, :], in_=earlier[:, :, :, :], compare_op=ALU.is_ge, fill=0.0,
                               base=-1, pattern=[[0, TT], [1, GROUPS], [-1, GROUPS]],
                               channel_multiplier=0).then_inc(const_ready, 1)
            heads = head_mask[:, :, :].rearrange("p c (h e) -> p c h e", e=HDIM)
            pool.affine_select(out=heads, in_=heads, compare_op=ALU.is_ge, fill=0.0, base=0,
                               pattern=[[0, KC], [-HDIM, P // HDIM], [0, HDIM]],
                               channel_multiplier=1).then_inc(const_step, 1)
            pool.wait_ge(const_step, 4)
            pool.affine_select(out=heads, in_=heads, compare_op=ALU.is_ge, fill=0.0, base=HDIM - 1,
                               pattern=[[0, KC], [HDIM, P // HDIM], [0, HDIM]],
                               channel_multiplier=-1).then_inc(const_ready, 1)
            pool.wait_ge(const_ready, 6)
            pool.wait_ge(small_loaded, 16 * 8)

            def rstd_of(ln):
                pool.wait_ge(mv_ready, ln + 1)
                pool.tensor_tensor(var_eps[:, :], mv[:, :, 1], eps[:, :], ALU.add).then_inc(var_eps_ready, 1)
                pool.wait_ge(var_eps_ready, ln + 1)
                pool.tensor_tensor(rstd[:, :], var_eps[:, :], minus_half[:, :], ALU.pow).then_inc(rstd_ready, 1)

            def split_lo(m):
                pool.wait_ge(we_hi_ready, m + 1)
                for s in range(2):
                    c = 2 * m + s
                    last = pool.tensor_tensor(we_lo[:, c, :], stage[:, s, :], we_hi[:, c, :], ALU.subtract)
                last.then_inc(we_lo_ready, 1)

            def x_plus_bias(b):
                pool.wait_ge(x_transposed, KC * (b + 1))
                for t in range(TT):
                    last = pool.tensor_tensor(x_all[:, b, t, :], x_in[:, t, :], b_o[:, :], ALU.add)
                last.then_inc(x_biased, 1)

            def batch(b, has_prev, early=None, mid=None, has_bias=True, sent=()):
                if has_prev:
                    rstd_of(b - 1)
                if early is not None:
                    split_lo(early)
                if has_bias:
                    x_plus_bias(b + 1)
                if mid is not None:
                    split_lo(mid)
                dispatch(sent)

            def dispatch(rows):
                for k, j in rows:
                    b, w = k // TT, k // WT
                    if k % WT == 0 and j == 0:
                        pool.wait_ge(slots_ready, w + 1)
                        pool.wait_ge(x1_kept, WB * (w + 1))
                        pool.wait_ge(zero_filled[w], 16 * FILLS)
                    pool.indirect_dma_start(xs_dram[w], bass.IndirectOffsetOnAxis(ap=slots[w][:, k % WT, j:j + 1], axis=0),
                                            x_all[:, b, k % TT, :], None).then_inc(dispatched[b], 16)

            def gather(k):
                w, i = k // WT, k % RING
                if k >= RING:
                    pool.wait_ge(combined, TOP_K * (k - RING + 1))
                for j in range(TOP_K):
                    pool.indirect_dma_start(y_got[i][:, j, :], None, ys_dram[w],
                                            bass.IndirectOffsetOnAxis(ap=slots[w][:, k % WT, j:j + 1], axis=0)
                                            ).then_inc(y_gathered[i], 16)

            SENT = (7, 30, 48)
            rows = [(k, j) for k in range(NB * TT) for j in range(TOP_K)]
            x_plus_bias(0)
            batch(0, False, early=0)
            batch(1, True, mid=1)
            with pool.Fori(2, 5) as b:
                batch(b, True, early=2 * b - 2, mid=2 * b - 1)
            batch(5, True, early=2 * 5 - 2, sent=rows[0:SENT[0]])
            batch(6, True, has_bias=False, sent=rows[SENT[0]:SENT[1]])
            batch(7, True, has_bias=False, sent=rows[SENT[1]:SENT[2]])
            rstd_of(NB - 1)
            dispatch(rows[SENT[2]:])
            pool.wait_ge(attended, KC * NB)
            pool.wait_ge(gated_ready, KC * NB)
            for w in range(WAVES):
                for r in range(RING):
                    pool.wait_ge(ys_stored[r], 16 * GROUPS_OF_PAIRS * (w + 1))
                for b in range(WB * w, WB * (w + 1)):
                    for t in range(TT):
                        gather(TT * b + t)
                        if b > 0 and t == (1 if w == 0 else TT - 1):
                            rstd_of(NB + b - 1)
            rstd_of(2 * NB - 1)

        @block.scalar
        def _(act):
            act.dma_start(b_q[:, :], bq.rearrange("(c p) -> p c", p=P), allow_slow_non_contiguous=True).then_inc(small_loaded, 16)
            act.dma_start(b_g[:, :], bg.rearrange("(c p) -> p c", p=P), allow_slow_non_contiguous=True).then_inc(small_loaded, 16)

            def xt_hi(b):
                for c in range(KC):
                    act.wait_ge(x_transposed, KC * b + c + 1)
                    act.activation(xT_hi[:, c, b, :], t_bank[c][:, :], ACT.Copy).then_inc(xt_hi_ready, 1)

            def x1t_hi(b):
                for c in range(KC):
                    act.wait_ge(x1_transposed, KC * b + c + 1)
                    act.activation(xT_hi[:, c, b, :], t_bank[c][:, :], ACT.Copy).then_inc(x1t_hi_ready, 1)

            def keep_x1(b):
                act.wait_ge(x1_ready, b + 1)
                act.activation(x_all[:, b, :, :], x1_sb[:, :, :], ACT.Copy).then_inc(x1_kept, 1)

            def split_hi(m):
                act.wait_ge(stage_loaded, 16 * 6 * (m + 1))
                act.activation(we_hi[:, 2 * m, :], stage[:, 0, :], ACT.Copy)
                act.activation(we_hi[:, 2 * m + 1, :], stage[:, 1, :], ACT.Copy).then_inc(we_hi_ready, 1)

            def routing_exp(b):
                act.wait_ge(gating_step, GATING_STEPS * b + 2)
                act.activation(r_exp[:, :, :], r_sub[:, :, :], ACT.Exp).then_inc(r_exp_ready, 1)

            def batch(b, prev, prev2, nxt, early=None, mid=None):
                if prev2:
                    routing_exp(b - 2)
                if early is not None:
                    split_hi(early)
                if nxt:
                    xt_hi(b + 1)
                act.wait_ge(small_loaded, 16 * 8)

                def q_parts(c):
                    act.wait_ge(q_projected, KC * b + c + 1)
                    if prev:
                        act.wait_ge(attended, KC * b)
                    act.activation(q_fm[:, c, :], qg_bank[c][:, :], ACT.Relu, bias=b_q[:, c:c + 1])
                    if prev:
                        act.wait_ge(q_ready, KC * b)
                    act.activation(q_exp[:, c, :], qg_bank[c][:, :], ACT.Exp, bias=b_q[:, c:c + 1]).then_inc(q_exp_ready, 1)

                q_parts(0)
                act.wait_ge(k_min_ready, b + 1)
                act.activation(k_min[:, :, :], k_min[:, :, :], ACT.Exp).then_inc(k_exp_ready, 1)
                q_parts(1)
                if prev:
                    x1t_hi(b - 1)
                if mid is not None:
                    split_hi(mid)
                if prev:
                    keep_x1(b - 1)
                for c in range(KC):
                    act.wait_ge(g_projected, KC * b + c + 1)
                    if prev:
                        act.wait_ge(gated_ready, KC * b)
                    act.activation(gate[:, c, :], qg_bank[c][:, :], ACT.Sigmoid, bias=b_g[:, c:c + 1]).then_inc(gate_ready, 1)

            xt_hi(0)
            act.wait_ge(wa_loaded, 16 * 4)
            act.activation(wa_hi[:, :, 0:2 * D], wa_stage[:, :, 0:2 * D], ACT.Copy).then_inc(wa_hi_ready, 1)
            act.activation(wa_hi[:, :, 2 * D:], wa_stage[:, :, 2 * D:], ACT.Copy).then_inc(wa_hi_ready, 1)
            act.wait_ge(gw_transposed, 1)
            act.activation(gwT_hi[:, :, :], y_bank[0][:, 0:KC * E].rearrange("p (c e) -> p c e", c=KC),
                           ACT.Copy).then_inc(gw_hi_ready, 1)
            batch(0, False, False, True, early=0)
            batch(1, True, False, True, mid=1)
            with act.Fori(2, 5) as b:
                batch(b, True, True, True, early=2 * b - 2, mid=2 * b - 1)
            batch(5, True, True, True, early=2 * 5 - 2)
            batch(6, True, True, True)
            batch(NB - 1, True, True, False)
            routing_exp(NB - 2)

            act.wait_ge(x_biased, NB)

            def shared(g):
                act.wait_ge(h1_ready, g + 1)
                if g > 0:
                    act.wait_ge(a_ready, g)
                act.activation(s_act, h_banks[g % 2][0][:, :], ACT.Silu).then_inc(silu_ready, 1)
                act.wait_ge(a_ready, g + 1)
                if g >= 2 * SHARED:
                    act.wait_ge(down_done, g // SHARED - 1)
                act.activation(a_hi[g % 4][:, :], a_act, ACT.Copy).then_inc(a_hi_ready, 1)

            shared(0)
            shared(1)
            x1t_hi(NB - 1)
            keep_x1(NB - 1)
            shared(2)
            routing_exp(NB - 1)
            for g in range(3, SHARED * EARLY):
                shared(g)

            def xst_hi(g, r):
                act.wait_ge(xs_transposed, g + 1)
                if late(g, 2):
                    act.wait_ge(h_ready, g - 1)
                act.activation(xsT_hi[r % 2][:, :, :], t_bank[r % 2][:, :].rearrange("p (c n) -> p c n", c=KC),
                               ACT.Copy).then_inc(xst_hi_ready, 1)

            def ys_copy(g, r, group):
                act.wait_ge(ys_ready, g + 1)
                if late(group, 1):
                    act.wait_ge(ys_stored[r], 16 * group)
                act.activation(ys[r][:, :, :], y_bank[r % 2][:, :].rearrange("p (t d) -> p t d", t=2),
                               ACT.Copy).then_inc(ys_copied, 1)

            def pair(g, r, ahead=True):
                if ahead:
                    xst_hi(g + 1, r + 1)
                act.wait_ge(h_ready, g + 1)
                if late(g, 1):
                    act.wait_ge(pair_a_ready, g)
                act.activation(s_pair[:, :], h_banks[r % 2][0][:, 0:2 * P], ACT.Silu).then_inc(pair_silu_ready, 1)
                act.wait_ge(pair_a_ready, g + 1)
                if late(g, 2):
                    act.wait_ge(ys_ready, g - 1)
                act.activation(aT_hi[r % 2][:, :], a_pair[:, :], ACT.Copy).then_inc(at_hi_ready, 1)

            def group(q, last=False):
                for r in range(RING):
                    pair(RING * q + r, r, not (last and r == RING - 1))
                    if r > 0:
                        ys_copy(RING * q + r - 1, r - 1, q)
                    elif late(q, 1):
                        ys_copy(RING * q - 1, RING - 1, q - 1)

            all_groups = WAVES * GROUPS_OF_PAIRS
            act.wait_ge(k_ready, NB)
            act.wait_ge(q_ready, KC * NB)
            xst_hi(0, 0)
            group(0)
            group(1)
            with act.Fori(1, all_groups // 2 - 1) as q2:
                group(2 * q2)
                group(2 * q2 + 1)
            group(all_groups - 2)
            group(all_groups - 1, last=True)
            ys_copy(RING * all_groups - 1, RING - 1, all_groups - 1)
            for g in range(SHARED * EARLY, SHARED * NB):
                shared(g)

        @block.vector
        def _(dve):
            def xt_lo(b):
                for c in range(KC):
                    dve.wait_ge(xt_hi_ready, KC * b + c + 1)
                    dve.tensor_tensor(xT_lo[:, c, b, :], t_bank[c][:, :], xT_hi[:, c, b, :],
                                      ALU.subtract).then_inc(xt_lo_ready, 1)

            def x1t_lo(b):
                for c in range(KC):
                    dve.wait_ge(x1t_hi_ready, KC * b + c + 1)
                    dve.tensor_tensor(xT_lo[:, c, b, :], t_bank[c][:, :], xT_hi[:, c, b, :],
                                      ALU.subtract).then_inc(x1t_lo_ready, 1)

            def kv_bias(b, t, prev):
                dve.wait_ge(kv_projected, TT * b + t + 1)
                if prev:
                    dve.wait_ge(kv_summed, b)
                dve.tensor_tensor(kv[:, t, :], kv_bank[t % 2][:, :], b_kv[:, :], ALU.add).then_inc(kv_biased, 1)

            def apply_gate(b, has_prev):
                for c in range(KC):
                    dve.wait_ge(attended, KC * b + c + 1)
                    dve.wait_ge(gate_ready, KC * b + c + 1)
                    if has_prev:
                        dve.wait_ge(wo_projected, 2 * b)
                    dve.tensor_tensor(gated[:, c, :], y_bank[c][:, :], gate[:, c, :], ALU.mult).then_inc(gated_ready, 1)

            def norm_stats(rows, ln):
                for t in range(TT):
                    last = dve.bn_stats(bn[:, t, :], rows(t))
                last.then_inc(bn_ready, 1)
                norm_moments(ln)

            def norm_moments(ln):
                dve.wait_ge(bn_ready, ln + 1)
                dve.memset(wait_pad[:, :], 0.0)
                for t in range(TT):
                    last = dve.bn_aggr(mv[:, t, :], bn[:, t, :])
                last.then_inc(mv_ready, 1)

            def x1_rows(t):
                return x1_sb[:, t, :]

            def x_plus_bias(b):
                dve.wait_ge(x_transposed, KC * (b + 1))
                dve.tensor_tensor(x_all[:, b, :, :], x_in[:, :, :],
                                  b_o[:, :].unsqueeze(1).to_broadcast([P, TT, D]), ALU.add).then_inc(x_biased, 1)

            def normalize(rows, outs, ln, done):
                dve.wait_ge(rstd_ready, ln + 1)
                for t in range(TT):
                    last = dve.tensor_scalar(outs(t), rows(t), mv[:, t, 0:1], rstd[:, t:t + 1],
                                             ALU.subtract, ALU.mult)
                last.then_inc(done, 1)

            def residual(b, has_prev):
                dve.wait_ge(x_biased, b + 1)
                if has_prev:
                    dve.wait_ge(x1_transposed, KC * b)
                    dve.wait_ge(x1_kept, b)
                for h in range(2):
                    dve.wait_ge(wo_projected, 2 * b + h + 1)
                    dve.tensor_tensor(x1_sb[:, 2 * h:2 * h + 2, :],
                                      y_bank[h][:, :].rearrange("p (t d) -> p t d", t=2),
                                      x_all[:, b, 2 * h:2 * h + 2, :], ALU.add).then_inc(residual_ready, 1)
                dve.wait_ge(residual_ready, 2 * b + 2)
                norm_stats(x1_rows, b)

            def routing_head(b):
                at = GATING_STEPS * b
                logits = t_bank[1][:, 0:TT * E].rearrange("p (t e) -> p t e", t=TT)
                per_tile = [P, TT, E]
                dve.wait_ge(logits_ready, b + 1)
                dve.tensor_reduce(r_max[:, :], logits, AX_X, ALU.max).then_inc(gating_step, 1)
                dve.wait_ge(gating_step, at + 1)
                dve.tensor_tensor(r_sub[:, :, :], logits, r_max[:, :].unsqueeze(2).to_broadcast(per_tile),
                                  ALU.subtract).then_inc(gating_step, 1)

            def routing_tail(b):
                at = GATING_STEPS * b
                per_tile = [P, TT, E]
                dve.wait_ge(r_exp_ready, b + 1)
                dve.tensor_reduce(r_sum[:, :], r_exp[:, :, :], AX_X, ALU.add).then_inc(gating_step, 1)
                dve.wait_ge(gating_step, at + 3)
                dve.reciprocal(r_inv[:, :], r_sum[:, :]).then_inc(gating_step, 1)
                dve.wait_ge(gating_step, at + 4)
                dve.tensor_tensor(score[:, :, :], r_exp[:, :, :], r_inv[:, :].unsqueeze(2).to_broadcast(per_tile),
                                  ALU.mult).then_inc(gating_step, 1)
                dve.wait_ge(gating_step, at + 5)
                grouped = score[:, :, :].rearrange("p t (g e) -> p t g e", g=GROUPS)
                dve.tensor_reduce(g_max[:, :, :], grouped, AX_X, ALU.max).then_inc(gating_step, 1)
                dve.wait_ge(gating_step, at + 6)
                pairs = [P, TT, GROUPS, GROUPS]
                other = g_max[:, :, :].unsqueeze(2).to_broadcast(pairs)
                own = g_max[:, :, :].unsqueeze(3).to_broadcast(pairs)
                dve.tensor_tensor(g_gt[:, :, :, :], other, own, ALU.is_gt)
                dve.tensor_tensor(g_eq[:, :, :, :], other, own, ALU.is_equal).then_inc(gating_step, 1)
                dve.wait_ge(gating_step, at + 7)
                dve.tensor_tensor(g_eq[:, :, :, :], g_eq[:, :, :, :], earlier[:, :, :, :], ALU.mult).then_inc(gating_step, 1)
                dve.wait_ge(gating_step, at + 8)
                dve.tensor_tensor(g_gt[:, :, :, :], g_gt[:, :, :, :], g_eq[:, :, :, :], ALU.add).then_inc(gating_step, 1)
                dve.wait_ge(gating_step, at + 9)
                dve.tensor_reduce(g_rank[:, :, :], g_gt[:, :, :, :], AX_X, ALU.add).then_inc(gating_step, 1)
                dve.wait_ge(gating_step, at + 10)
                dve.tensor_scalar(g_sel[:, :, :], g_rank[:, :, :], float(TOP_GROUPS), None, ALU.is_lt).then_inc(gating_step, 1)
                dve.wait_ge(gating_step, at + 11)
                dve.tensor_tensor(masked[:, :, 0:E].rearrange("p t (g e) -> p t g e", g=GROUPS), grouped,
                                  g_sel[:, :, :].unsqueeze(3).to_broadcast([P, TT, GROUPS, EG]),
                                  ALU.mult).then_inc(gating_step, 1)
                dve.wait_ge(gating_step, at + 12)
                dve.memset(wait_pad[:, :], 0.0)
                for t in range(TT):
                    last = dve.max(top8[:, t, :], masked[:, t, 0:E])
                last.then_inc(gating_step, 1)
                dve.wait_ge(gating_step, at + 13)
                dve.memset(top8[:, :, TOP_K:], FILLER).then_inc(gating_step, 1)
                dve.wait_ge(gating_step, at + 14)
                dve.memset(wait_pad[:, :], 0.0)
                for t in range(TT):
                    last = dve.match_replace(marked[:, t, :], top8[:, t, :], masked[:, t, :], TAKEN)
                last.then_inc(gating_step, 1)
                dve.wait_ge(gating_step, at + 15)
                dve.tensor_scalar(sel_all[:, b, :, :], marked[:, :, 0:E], TAKEN, None, ALU.is_equal)
                dve.scalar_tensor_tensor(c_all[:, b, :, :], marked[:, :, 0:E], TAKEN, score[:, :, :],
                                         ALU.is_equal, ALU.mult).then_inc(c_ready, 1)

            def plan_copy(w):
                dve.wait_ge(counted, w + 1)
                dve.tensor_copy(prefix[:, :], count_bank[w][:, 0:(WT + 1) * E]).then_inc(plan_copied, 1)

            def plan_tokens(w, parts=range(PLAN_PARTS)):
                at = PLAN_STEPS * w
                by_tile = [P, WT, E]
                total = prefix[:, WT * E:]
                over = work[:, 0:E * MOST].rearrange("p (e j) -> p e j", e=E)
                ahead = work[:, 0:E * E].rearrange("p (e f) -> p e f", e=E)
                ended = work[0:1, 0:NPAIR * E].rearrange("p (g e) -> p g e", g=NPAIR)
                if 0 in parts:
                    dve.wait_ge(plan_copied, w + 1)
                    dve.wait_ge(we_lo_ready, PAIRS)
                    dve.tensor_tensor(over, total.unsqueeze(2).to_broadcast([P, E, MOST]),
                                      starts.unsqueeze(1).to_broadcast([P, E, MOST]), ALU.is_gt).then_inc(plan_step, 1)
                if 1 in parts:
                    dve.wait_ge(plan_step, at + 1)
                    dve.tensor_reduce(n_pairs[:, :], over, AX_X, ALU.add).then_inc(plan_step, 1)
                if 2 in parts:
                    dve.wait_ge(plan_step, at + 2)
                    dve.tensor_tensor(ahead, n_pairs[:, :].unsqueeze(1).to_broadcast([P, E, E]), earlier_e,
                                      ALU.mult).then_inc(plan_step, 1)
                if 3 in parts:
                    dve.wait_ge(plan_step, at + 3)
                    dve.tensor_reduce(first_pair[:, :], ahead, AX_X, ALU.add).then_inc(plan_step, 1)
                if 4 in parts:
                    dve.wait_ge(plan_step, at + 4)
                    dve.tensor_scalar(first_slot[:, :], first_pair[:, :], float(PAIR), 1.0, ALU.mult, ALU.add).then_inc(plan_step, 1)
                if 5 in parts:
                    dve.wait_ge(plan_step, at + 5)
                    dve.tensor_tensor(slot_of[w][:, :, :], prefix[:, 0:WT * E].rearrange("p (t e) -> p t e", t=WT),
                                      first_slot[:, :].unsqueeze(1).to_broadcast(by_tile), ALU.add).then_inc(plan_step, 1)
                if 6 in parts:
                    dve.wait_ge(plan_step, at + 6)
                    dve.tensor_tensor(slot_of[w][:, :, :], slot_of[w][:, :, :],
                                      sel_all[:, WB * w:WB * (w + 1), :, :].rearrange("p b t e -> p (b t) e"),
                                      ALU.mult).then_inc(plan_step, 1)
                if 7 in parts:
                    dve.wait_ge(plan_step, at + 7)
                for quarter in range(4):
                    if 7 + quarter in parts:
                        for t in range(WT // 4 * quarter, WT // 4 * (quarter + 1)):
                            last = dve.max(slot8[w][:, t, :], slot_of[w][:, t, :])
                        if quarter == 3:
                            last.then_inc(plan_step, 1)
                if 11 in parts:
                    dve.wait_ge(plan_step, at + 8)
                    dve.tensor_scalar(slots[w][:, :, :], slot8[w][:, :, 0:TOP_K], 1.0, None, ALU.subtract).then_inc(slots_ready, 1)
                    dve.tensor_tensor(pairs_end[:, :], first_pair[:, :], n_pairs[:, :], ALU.add).then_inc(plan_step, 1)
                if 12 in parts:
                    dve.wait_ge(plan_step, at + 9)
                    dve.tensor_tensor(ended, pair_no[0:1, :].unsqueeze(2).to_broadcast([1, NPAIR, E]),
                                      pairs_end[0:1, :].unsqueeze(1).to_broadcast([1, NPAIR, E]), ALU.is_ge).then_inc(plan_step, 1)
                if 13 in parts:
                    dve.wait_ge(plan_step, at + 10)
                    dve.tensor_reduce(pair_expert_f[:, :], ended, AX_X, ALU.add).then_inc(plan_step, 1)
                if 14 in parts:
                    dve.wait_ge(plan_step, at + 11)
                    dve.tensor_scalar(pair_expert_f[:, :], pair_expert_f[:, :], float(E - 1), float(SHARED),
                                      ALU.min, ALU.add).then_inc(plan_step, 1)
                if 15 in parts:
                    dve.wait_ge(plan_step, at + 12)
                    dve.tensor_copy(pair_chunk[:, NPAIR * w:NPAIR * (w + 1), 0], pair_expert_f[:, :]).then_inc(experts_ready, 1)
                for h in range(2):
                    rows = slice(WT // 2 * h, WT // 2 * (h + 1))
                    tiles = c_all[:, WB * w + WB // 2 * h:WB * w + WB // 2 * (h + 1), :, :].rearrange("p b t e -> p (b t) e")
                    by_slot = [P, WT // 2, TOP_K, E]
                    match = work[:, 0:WT // 2 * TOP_K * E].rearrange("p (t k e) -> p t k e", t=WT // 2, k=TOP_K)
                    part, step = 16 + 3 * h, 4 * w + 2 * h
                    if part in parts:
                        if h == 0:
                            dve.wait_ge(experts_ready, w + 1)
                        else:
                            dve.wait_ge(c_of_slot_ready, 2 * w + 1)
                        dve.tensor_tensor(match, slot_of[w][:, rows, :].unsqueeze(2).to_broadcast(by_slot),
                                          slot8[w][:, rows, 0:TOP_K].unsqueeze(3).to_broadcast(by_slot),
                                          ALU.is_equal).then_inc(weight_step, 1)
                    if part + 1 in parts:
                        dve.wait_ge(weight_step, step + 1)
                        dve.tensor_tensor(match, match, tiles.unsqueeze(2).to_broadcast(by_slot),
                                          ALU.mult).then_inc(weight_step, 1)
                    if part + 2 in parts:
                        dve.wait_ge(weight_step, step + 2)
                        dve.tensor_reduce(c_of_slot[w][:, rows, :], match, AX_X, ALU.add).then_inc(c_of_slot_ready, 1)

            def batch(b, prev, prev2, nxt, plan=None):
                if prev:
                    apply_gate(b - 1, prev2)
                kv_bias(b, 0, prev)
                kv_bias(b, 1, prev)
                if plan == "slots":
                    routing_tail(b - 2)
                if prev:
                    residual(b - 1, prev2)
                kv_bias(b, 2, prev)
                kv_bias(b, 3, prev)
                dve.wait_ge(kv_biased, TT * (b + 1))
                dve.tensor_scalar(k_min[:, :, :], kv[:, :, 0:D], 0.0, None, ALU.min).then_inc(k_min_ready, 1)
                if plan == "slots":
                    plan_copy(0)
                if prev:
                    normalize(x1_rows, x1_rows, b - 1, x1_ready)
                if nxt:
                    xt_lo(b + 1)
                if isinstance(b, int) and b == NB - 1:
                    x_plus_bias(b)

                def q_elu(c):
                    dve.wait_ge(q_exp_ready, KC * b + c + 1)
                    dve.scalar_tensor_tensor(q_fm[:, c, :], q_exp[:, c, :], 1.0, q_fm[:, c, :],
                                             ALU.min, ALU.add).then_inc(q_ready, 1)

                q_elu(0)
                dve.wait_ge(k_exp_ready, b + 1)
                dve.scalar_tensor_tensor(kv[:, :, 0:D], kv[:, :, 0:D], 0.0, k_min[:, :, :],
                                         ALU.max, ALU.add).then_inc(k_ready, 1)
                q_elu(1)
                if prev:
                    x1t_lo(b - 1)
                dve.wait_ge(kv_summed, b + 1)
                if prev:
                    dve.wait_ge(attended, KC * b)
                dve.tensor_tensor(kv_heads[:, :, :], kv_bank[0][:, 0:KC * P].rearrange("p (c n) -> p c n", c=KC),
                                  head_mask[:, :, :], ALU.mult).then_inc(kv_heads_ready, 1)
                if prev2 and plan != "slots":
                    routing_tail(b - 2)
                if prev:
                    routing_head(b - 1)
                if plan == "slots":
                    plan_tokens(0, range(SLOTS_READY_PART))
                if plan == "experts":
                    plan_tokens(0, range(SLOTS_READY_PART, WEIGHTS_PART))

            xt_lo(0)
            for k in range(2):
                half = slice(2 * D * k, 2 * D * (k + 1))
                dve.wait_ge(wa_hi_ready, k + 1)
                dve.tensor_tensor(wa_lo[:, :, half], wa_stage[:, :, half], wa_hi[:, :, half],
                                  ALU.subtract).then_inc(wa_lo_ready, 1)
            dve.wait_ge(const_ready, 6)
            dve.wait_ge(small_loaded, 16 * 8)
            dve.wait_ge(gw_hi_ready, 1)
            dve.tensor_tensor(gwT_lo[:, :, :], y_bank[0][:, 0:KC * E].rearrange("p (c e) -> p c e", c=KC),
                              gwT_hi[:, :, :], ALU.subtract).then_inc(gw_lo_ready, 1)
            dve.tensor_copy(before[:, :], before_f).then_inc(count_consts_ready, 1)
            dve.memset(ones[:, :], 1.0).then_inc(count_consts_ready, 1)
            dve.wait_ge(wa_lo_ready, 2)
            dve.memset(wa_flat[:, :], 0.0).then_inc(zeros_ready, 1)
            batch(0, False, False, True)
            batch(1, True, False, True)
            with dve.Fori(2, 5) as b:
                batch(b, True, True, True)
            batch(5, True, True, True, plan="slots")
            batch(6, True, True, True, plan="experts")
            batch(7, True, True, False)
            apply_gate(NB - 1, True)

            def shared_hidden(g, add=None):
                dve.wait_ge(silu_ready, g + 1)
                dve.wait_ge(h3_ready, g + 1)
                if g > 0:
                    dve.wait_ge(a_lo_ready, g)
                dve.tensor_tensor(a_act, h_banks[g % 2][1][:, :], s_act, ALU.mult).then_inc(a_ready, 1)
                if add:
                    combine(1, *add, 0, whole=False)
                dve.wait_ge(a_hi_ready, g + 1)
                dve.tensor_tensor(a_lo[g % 4][:, :], a_act, a_hi[g % 4][:, :], ALU.subtract).then_inc(a_lo_ready, 1)
                if add:
                    for j in range(1, TOP_K):
                        combine(1, *add, j, whole=False)

            def add_shared(n, tiles_seen=0):
                dve.wait_ge(dispatched[n], 16 * TT * TOP_K)
                dve.wait_ge(down_done, n + 1)
                if tiles_seen:
                    dve.wait_ge(combined, TOP_K * tiles_seen)
                for h in range(2):
                    last = dve.tensor_tensor(x_all[:, n, 2 * h:2 * h + 2, :],
                                             y_bank[h][:, :].rearrange("p (t d) -> p t d", t=2),
                                             x_all[:, n, 2 * h:2 * h + 2, :], ALU.add)
                last.then_inc(shared_added, 1)

            shared_hidden(0)
            residual(NB - 1, True)
            shared_hidden(1)
            normalize(x1_rows, x1_rows, NB - 1, x1_ready)
            routing_tail(NB - 2)
            x1t_lo(NB - 1)
            shared_hidden(2)
            routing_head(NB - 1)
            shared_hidden(3)
            add_shared(0)
            shared_hidden(4)
            shared_hidden(5)
            add_shared(1)
            routing_tail(NB - 1)
            add_shared(2)

            def xst_lo(g, r):
                dve.wait_ge(xst_hi_ready, g + 1)
                dve.tensor_tensor(xsT_lo[r % 2][:, :, :], t_bank[r % 2][:, :].rearrange("p (c n) -> p c n", c=KC),
                                  xsT_hi[r % 2][:, :, :], ALU.subtract).then_inc(xst_lo_ready, 1)

            def pair(g, r, ahead=True, add=None, norm=None, whole=True, part=None):
                if ahead:
                    xst_lo(g + 1, r + 1)
                dve.wait_ge(pair_silu_ready, g + 1)
                if late(g, 1):
                    dve.wait_ge(at_lo_ready, g)
                dve.tensor_tensor(a_pair, h_banks[r % 2][0][:, 2 * P:], s_pair, ALU.mult).then_inc(pair_a_ready, 1)
                if add:
                    b, t, j = add
                    combine(0, b, t, j, whole)
                if norm is not None:
                    final_norm(norm, r)
                if part:
                    plan_tokens(part[0], [part[1]])
                dve.wait_ge(at_hi_ready, g + 1)
                dve.tensor_tensor(aT_lo[r % 2][:, :], a_pair, aT_hi[r % 2][:, :], ALU.subtract).then_inc(at_lo_ready, 1)
                if add:
                    combine(0, b, t, j + 1, whole)

            def combine(w, b, t, j, whole=True):
                if j == 0:
                    dve.wait_ge(y_gathered[t], 16 * TOP_K * (b + 1))
                if late(b, 1) or t > 0 or j > 0:
                    dve.wait_ge(combined, TOP_K * (TT * b + t) + j)
                weight = c_of_slot[w][:, TT * (b - WB * w) + t, j:j + 1]
                dve.scalar_tensor_tensor(x_all[:, b, t, :], y_got[t][:, j, :], weight, x_all[:, b, t, :],
                                         ALU.mult, ALU.add).then_inc(combined, 1)
                if j == TOP_K - 1 and whole:
                    dve.wait_ge(combined, TOP_K * (TT * b + t + 1))
                    dve.memset(wait_pad[:, :], 0.0)
                    last = dve.bn_stats(bn[:, t, :], x_all[:, b, t, :])
                    if t == TT - 1:
                        last.then_inc(bn_ready, 1)
                        norm_moments(NB + b)

            def final_norm(b, t):
                if t == 0:
                    dve.wait_ge(rstd_ready, NB + b + 1)
                    if late(b, 1):
                        dve.wait_ge(out_stored, 16 * b)
                last = dve.tensor_scalar(o_sb[:, t, :], x_all[:, b, t, :], mv[:, t, 0:1], rstd[:, t:t + 1],
                                         ALU.subtract, ALU.mult)
                if t == TT - 1:
                    last.then_inc(out_ready, 1)

            def group(q, adds=None, norm=None, whole=True, parts=(), last=False):
                for r in range(RING):
                    add = (adds[0], adds[1] + r // 2, 2 * (r % 2)) if adds else None
                    pair(RING * q + r, r, not (last and r == RING - 1), add, norm, whole,
                         parts[r] if r < len(parts) else None)

            q1 = GROUPS_OF_PAIRS
            xst_lo(0, 0)
            plan_copy(1)
            group(0)
            parts = [(1, k) for k in range(WEIGHTS_PART)] + [(w, k) for w in range(WAVES) for k in range(WEIGHTS_PART, PLAN_PARTS)]
            for q in range(1, PLAN_GROUPS + 1):
                group(q, parts=parts[RING * (q - 1):RING * q])
            with dve.Fori(PLAN_GROUPS // 2 + 1, q1 // 2 + 1) as q2:
                group(2 * q2)
                group(2 * q2 + 1)
            dve.wait_ge(c_of_slot_ready, 2 * WAVES)
            dve.wait_ge(shared_added, EARLY)
            group(q1 + 2, (0, 0))
            group(q1 + 3, (0, 2))
            with dve.Fori(1, EARLY) as b:
                group(q1 + 2 + 2 * b, (b, 0), norm=b - 1)
                group(q1 + 3 + 2 * b, (b, 2))
            group(q1 + 2 + 2 * EARLY, (EARLY, 0), norm=EARLY - 1, whole=False)
            group(q1 + 3 + 2 * EARLY, (EARLY, 2), whole=False)
            group(q1 + 2 + 2 * WB)
            group(WAVES * q1 - 1, last=True)

            tiles = [(b, t) for b in range(WB, NB) for t in range(TT)]

            def whole_stats(b):
                norm_stats(lambda t: x_all[:, b, t, :], NB + b)

            def whole_norm(b):
                for t in range(TT):
                    final_norm(b, t)

            for par in range(SHARED):
                shared_hidden(SHARED * EARLY + par)
            for n in range(WB, NB):
                at = 2 * (n - WB)
                shared_hidden(SHARED * n, tiles[at])
                shared_hidden(SHARED * n + 1, tiles[at + 1])
                add_shared(n - 1, WT + at + 2)
                dve.wait_ge(shared_added, n)
                if n in (WB + 1, WB + 2):
                    whole_norm(n - 2)
                if n < WB + 2:
                    whole_stats(n - 1)
            whole_stats(WB + 1)
            add_shared(NB - 1, WT + 2 * WB)
            dve.wait_ge(shared_added, NB)
            for b in range(WB + 2, NB):
                for t in range(TT):
                    for j in range(TOP_K):
                        combine(1, b, t, j)
                    if t == 2:
                        whole_norm(b - 1)
            whole_norm(NB - 1)

        @block.tensor
        def _(pe):
            def product(dst, sta_hi, sta_lo, mov_hi, mov_lo, start, stop):
                pe.matmul(dst, sta_hi, mov_hi, start=start, stop=False)
                pe.matmul(dst, sta_hi, mov_lo, start=False, stop=False)
                return pe.matmul(dst, sta_lo, mov_hi, start=False, stop=stop)

            def transpose_x(src, done):
                for c in range(KC):
                    for t in range(TT):
                        last = pe.transpose(t_bank[c][:, t * P:(t + 1) * P], src[:, t, c * P:(c + 1) * P],
                                            ident[:, :])
                    last.then_inc(done, 1)

            def project_kv(b, t):
                if not (isinstance(b, int) and b == 0) or t >= 2:
                    pe.wait_ge(kv_biased, TT * b + t - 1)
                if not (isinstance(b, int) and b == 0) and t == 0:
                    pe.wait_ge(kv_heads_ready, b)
                tok = slice(t * P, (t + 1) * P)
                for c in range(KC):
                    last = product(kv_bank[t % 2][:, :], xT_hi[:, c, b, tok], xT_lo[:, c, b, tok],
                                   wa_hi[:, c, 0:2 * D], wa_lo[:, c, 0:2 * D], c == 0, c == KC - 1)
                last.then_inc(kv_projected, 1)

            def project_features(b, m, col, done):
                cols = slice(col + m * P, col + (m + 1) * P)
                for c in range(KC):
                    last = product(qg_bank[m][:, :], wa_hi[:, c, cols], wa_lo[:, c, cols],
                                   xT_hi[:, c, b, :], xT_lo[:, c, b, :], c == 0, c == KC - 1)
                last.then_inc(done, 1)

            def project_out(b):
                for h in range(2):
                    pe.wait_ge(gated_ready, KC * (b + 1))
                    for t in range(2 * h, 2 * h + 2):
                        for c in range(KC):
                            last = pe.matmul(y_bank[h][:, (t % 2) * D:(t % 2 + 1) * D],
                                             gated[:, c, t * P:(t + 1) * P], wo_sb[:, c, :],
                                             start=c == 0, stop=c == KC - 1)
                    last.then_inc(wo_projected, 1)

            def sum_kv(b):
                pe.wait_ge(k_ready, b + 1)
                for c in range(KC):
                    for t in range(TT):
                        last = pe.matmul(kv_bank[0][:, c * P:(c + 1) * P], kv[:, t, c * P:(c + 1) * P],
                                         kv[:, t, D + c * P:D + (c + 1) * P], start=t == 0, stop=t == TT - 1)
                last.then_inc(kv_summed, 1)

            def attend(b):
                pe.wait_ge(kv_heads_ready, b + 1)
                pe.wait_ge(q_ready, KC * (b + 1))
                for c in range(KC):
                    pe.matmul(y_bank[c][:, :], kv_heads[:, c, :], q_fm[:, c, :], start=True,
                              stop=True).then_inc(attended, 1)

            def route(b):
                pe.wait_ge(x1t_lo_ready, KC * (b + 1))
                for t in range(TT):
                    dst = t_bank[1][:, t * E:(t + 1) * E]
                    for c in range(KC):
                        hi, lo = xT_hi[:, c, b, t * P:(t + 1) * P], xT_lo[:, c, b, t * P:(t + 1) * P]
                        pe.matmul(dst, hi, gwT_hi[:, c, :], start=c == 0, stop=False)
                        pe.matmul(dst, hi, gwT_lo[:, c, :], start=False, stop=False)
                        pe.matmul(dst, lo, gwT_hi[:, c, :], start=False, stop=False)
                        last = pe.matmul(dst, lo, gwT_lo[:, c, :], start=False, stop=c == KC - 1)
                last.then_inc(logits_ready, 1)

            def count_tokens(w):
                pe.wait_ge(count_consts_ready, 2)
                pe.wait_ge(c_ready, WB * (w + 1))
                counts = count_bank[w][:, 0:(WT + 1) * E].rearrange("p (t e) -> p t e", e=E)
                chosen = sel_all[:, WB * w:WB * (w + 1), :, :].rearrange("p b t e -> p (b t) e")
                pe.matmul(counts[:, 0:WT, :], before[:, :], chosen, start=True, stop=False)
                for u in range(WT - 1):
                    pe.matmul(counts[:, u + 1:WT, :], ones[:, :],
                              chosen[:, u:u + 1, :].to_broadcast([P, WT - 1 - u, E]), start=False, stop=u == WT - 2)
                for u in range(WT):
                    last = pe.matmul(counts[:, WT, :], ones[:, :], chosen[:, u, :], start=u == 0, stop=u == WT - 1)
                last.then_inc(counted, 1)

            def batch(b, prev, prev2, nxt, plan=False):
                pe.wait_ge(xt_lo_ready, KC * (b + 1))
                project_kv(b, 0)
                project_kv(b, 1)
                if prev:
                    project_out(b - 1)
                project_kv(b, 2)
                project_kv(b, 3)
                if plan:
                    pe.wait_ge(x1t_lo_ready, KC * (b - 1))
                    count_tokens(0)
                if nxt:
                    pe.wait_ge(x_loaded, 16 * (b + 2))
                if prev2:
                    pe.wait_ge(x1t_lo_ready, KC * (b - 1))
                    if plan:
                        pe.wait_ge(plan_copied, 1)
                    pe.wait_ge(gating_step, GATING_STEPS * (b - 2) + 2)
                if nxt:
                    transpose_x(x_in, x_transposed)
                if prev:
                    pe.wait_ge(gate_ready, KC * b)
                project_features(b, 0, 2 * D, q_projected)
                project_features(b, 1, 2 * D, q_projected)
                if nxt:
                    pe.wait_ge(xt_lo_ready, KC * (b + 2))
                if prev:
                    pe.wait_ge(x1_ready, b)
                    transpose_x(x1_sb, x1_transposed)
                pe.wait_ge(q_exp_ready, KC * b + 1)
                project_features(b, 0, 3 * D, g_projected)
                sum_kv(b)
                pe.wait_ge(q_exp_ready, KC * b + 2)
                project_features(b, 1, 3 * D, g_projected)
                if prev:
                    route(b - 1)
                    pe.wait_ge(residual_ready, 2 * b)
                attend(b)

            pe.wait_ge(const_ready, 6)
            pe.wait_ge(x_loaded, 16)
            transpose_x(x_in, x_transposed)
            pe.wait_ge(small_loaded, 16 * 8)
            for c in range(KC):
                last = pe.transpose(y_bank[0][:, c * E:(c + 1) * E], gw_sb[:, c * P:(c + 1) * P], ident[0:E, 0:E])
            last.then_inc(gw_transposed, 1)
            pe.wait_ge(wa_lo_ready, 2)
            pe.wait_ge(gw_lo_ready, 1)
            batch(0, False, False, True)
            batch(1, True, False, True)
            with pe.Fori(2, 5) as b:
                batch(b, True, True, True)
            batch(5, True, True, True, plan=True)
            batch(6, True, True, True)
            batch(NB - 1, True, True, False)

            def up(g, n, par):
                if late(g, 2):
                    pe.wait_ge(a_ready, g - 1)
                for k, done in enumerate((h1_ready, h3_ready)):
                    for c in range(KC):
                        cols = slice((c * 2 + k) * INTER, (c * 2 + k + 1) * INTER)
                        last = product(h_banks[par][k][:, :], we_hi[:, par, cols], we_lo[:, par, cols],
                                       xT_hi[:, c, n, :], xT_lo[:, c, n, :], c == 0, c == KC - 1)
                    last.then_inc(done, 1)

            def down(n):
                pe.wait_ge(a_lo_ready, SHARED * (n + 1))
                if late(n, 1):
                    pe.wait_ge(shared_added, n)
                at = 2 * (n % 2)
                for t in range(TT):
                    tok = slice(t * P, (t + 1) * P)
                    for j in range(SHARED):
                        last = product(y_bank[t // 2][:, (t % 2) * D:(t % 2 + 1) * D], a_hi[at + j][:, tok], a_lo[at + j][:, tok],
                                       we_hi[:, j, W13:], we_lo[:, j, W13:], j == 0, j == SHARED - 1)
                last.then_inc(down_done, 1)

            pe.wait_ge(we_lo_ready, PAIRS)
            pe.wait_ge(kv_biased, TT * NB)
            pe.wait_ge(kv_heads_ready, NB)
            up(0, 0, 0)
            project_out(NB - 1)
            pe.wait_ge(gate_ready, KC * NB)
            up(1, 0, 1)
            up(2, 1, 0)
            pe.wait_ge(x1_ready, NB)
            pe.wait_ge(x1t_lo_ready, KC * (NB - 1))
            pe.wait_ge(gating_step, GATING_STEPS * (NB - 2) + 2)
            transpose_x(x1_sb, x1_transposed)
            up(3, 1, 1)
            route(NB - 1)
            pe.wait_ge(residual_ready, 2 * NB)
            down(0)
            up(4, 2, 0)
            up(5, 2, 1)
            down(1)
            down(2)

            def transpose_xs(g, r, use):
                pe.wait_ge(xs_loaded[r], 16 * use)
                for c in range(KC):
                    for i in range(2):
                        last = pe.transpose(t_bank[r % 2][:, c * 2 * P + i * P:c * 2 * P + (i + 1) * P],
                                            xs[r][:, i, c * P:(c + 1) * P], ident[:, :])
                last.then_inc(xs_transposed, 1)

            def chunk_of(g):
                return pe.value_load(pair_chunk[0:1, g, :], min_val=SHARED, max_val=NCH - 1)

            def up_pair(g, r, chunk):
                pe.wait_ge(xst_lo_ready, g + 1)
                for k in range(2):
                    for c in range(KC):
                        cols = slice((c * 2 + k) * INTER, (c * 2 + k + 1) * INTER)
                        last = product(h_banks[r % 2][0][:, k * PAIR:(k + 1) * PAIR],
                                       we_hi[:, chunk, cols], we_lo[:, chunk, cols],
                                       xsT_hi[r % 2][:, c, :], xsT_lo[r % 2][:, c, :], c == 0, c == KC - 1)
                last.then_inc(h_ready, 1)

            def down_pair(g, r, chunk):
                pe.wait_ge(at_lo_ready, g + 1)
                if late(g, 2):
                    pe.wait_ge(ys_copied, g - 1)
                w2_hi, w2_lo = we_hi[:, chunk, W13:], we_lo[:, chunk, W13:]
                dst, tok = y_bank[r % 2][:, 0:D], slice(0, P)
                pe.matmul(dst, aT_hi[r % 2][:, tok], w2_hi, start=True, stop=False)
                pe.matmul(dst, aT_lo[r % 2][:, tok], w2_hi, start=False, stop=False)
                pe.matmul(dst, aT_hi[r % 2][:, tok], w2_lo, start=False, stop=True)
                dst, tok = y_bank[r % 2][:, D:], slice(P, PAIR)
                pe.matmul(dst, aT_hi[r % 2][:, tok], w2_lo, start=True, stop=False)
                pe.matmul(dst, aT_hi[r % 2][:, tok], w2_hi, start=False, stop=False)
                pe.matmul(dst, aT_lo[r % 2][:, tok], w2_hi, start=False, stop=True).then_inc(ys_ready, 1)

            def two_groups(q, last=False):
                for i in range(2 * RING):
                    g, r = RING * q + i, i % RING
                    if not (last and i == 2 * RING - 1):
                        transpose_xs(g + 1, (r + 1) % RING, q + 1 + (i + 1) // RING)
                    if i > 0:
                        before_this = chunk
                    chunk = chunk_of(g)
                    up_pair(g, r, chunk)
                    if i == 0 and late(q, 1):
                        before_this = chunk_of(g - 1)
                    if i > 0 or late(q, 1):
                        down_pair(g - 1, (r - 1) % RING, before_this)
                return chunk

            all_groups = WAVES * GROUPS_OF_PAIRS
            pe.wait_ge(experts_ready, 1)
            pe.wait_ge(x1t_lo_ready, KC * NB)
            pe.wait_ge(gating_step, GATING_STEPS * (NB - 1) + 2)
            transpose_xs(0, 0, 1)
            pe.wait_ge(a_ready, SHARED * EARLY)
            count_tokens(1)
            pe.wait_ge(shared_added, EARLY)
            two_groups(0)
            with pe.Fori(1, GROUPS_OF_PAIRS // 2) as q2:
                two_groups(2 * q2)
            pe.wait_ge(experts_ready, 2)
            with pe.Fori(GROUPS_OF_PAIRS // 2, all_groups // 2 - 1) as q2:
                two_groups(2 * q2)
            chunk = two_groups(all_groups - 2, last=True)
            pe.wait_ge(pair_a_ready, RING * all_groups - 1)
            pe.wait_ge(plan_copied, WAVES)
            up(SHARED * EARLY, EARLY, 0)
            down_pair(RING * all_groups - 1, RING - 1, chunk)
            pe.wait_ge(pair_a_ready, RING * all_groups)
            up(SHARED * EARLY + 1, EARLY, 1)
            pe.wait_ge(ys_copied, RING * all_groups)
            for n in range(EARLY + 1, NB):
                up(SHARED * n, n, 0)
                up(SHARED * n + 1, n, 1)
                down(n - 1)
            down(NB - 1)


_INS = ["L0_attn_x", "L0_attn_Wq", "L0_attn_bq", "L0_attn_Wk", "L0_attn_bk", "L0_attn_Wv", "L0_attn_bv",
        "L0_attn_Wg", "L0_attn_bg", "L0_attn_Wo", "L0_attn_bo", "L0_ffn_gate_w", "L0_ffn_w1", "L0_ffn_w2",
        "L0_ffn_w3", "L0_ffn_ws1", "L0_ffn_ws2", "L0_ffn_ws3"]


def _plan_constants(np, token_tiles, experts):
    pairs = token_tiles * TOP_K // 2 + experts
    before = np.triu(np.ones((P, P)), 1)
    earlier_e = np.tril(np.ones((experts, experts)), -1).reshape(1, -1)
    starts = 2 * P * np.arange(token_tiles // 2).reshape(1, -1)
    pair_no = np.arange(pairs).reshape(1, -1)
    rows = [np.broadcast_to(a, (P, a.shape[1])) for a in (before, earlier_e, starts, pair_no)]
    return np.concatenate(rows, axis=1).astype(np.float32)


def kernel(**inputs):
    import numpy as _np
    import concourse.bacc as _bacc
    from concourse.bass_utils import run_bass_kernel_spmd as _run

    nc = _bacc.Bacc("TRN2", target_bir_lowering=False, num_devices=1)
    arrays, args = {}, []
    tokens_sent = inputs["L0_attn_x"].shape[0] * inputs["L0_attn_x"].shape[1] // 2
    experts = inputs["L0_ffn_gate_w"].shape[0]
    sources = dict(inputs, plan_consts=_plan_constants(_np, tokens_sent // P, experts))
    for name in _INS + ["plan_consts"]:
        a = _np.ascontiguousarray(sources[name])
        arrays[f"in_{name}"] = a
        args.append(nc.dram_tensor(f"in_{name}", a.shape, mybir.dt.from_np(a.dtype), kind="ExternalInput").ap())
    shape = arrays["in_L0_attn_x"].shape
    args.append(nc.dram_tensor("out_0", shape, F32, kind="ExternalOutput").ap())
    attention_and_experts(nc, *args)
    r = _run(nc, [arrays], core_ids=[0])
    return r.results[0]["out_0"]
```
